# Optimizing a Trainium2 kernel written in Bass

```python
import numpy as np
import jax
import jax.numpy as jnp

def _softmax(x, axis=-1):
    return jax.nn.softmax(x, axis=axis)

def _gelu(x):
    return jax.nn.gelu(x, approximate=True)

def _silu(x):
    return jax.nn.silu(x)

def _sigmoid(x):
    return jax.nn.sigmoid(x)

def _layernorm(x, axis=-1, eps=1e-05):
    m = jnp.mean(x, axis=axis, keepdims=True)
    v = jnp.var(x, axis=axis, keepdims=True)
    return (x - m) / jnp.sqrt(v + eps)

def _scatter_add(tgt, idx, src, axis=0):
    return tgt.at[idx].add(src)

def _segment_sum(src, seg, n):
    return jax.ops.segment_sum(src, seg, n)
kernel_name = 'mk_seq_postln_d1_jaxref_r2_4afa4a'

def setup_inputs(seed: int=0):
    np.random.seed(seed)
    _w = jnp.asarray

    def _L0_attn_setup():
        import jax, jax.numpy as jnp
        import numpy as np
        B, S, DIM, H = (2, 1024, 512, 16)
        D = DIM // H

        def _xavier(key, shape):
            a = float(np.sqrt(6.0 / (shape[0] + shape[1])))
            return jax.random.uniform(key, shape, minval=-a, maxval=a, dtype=jnp.float32)

        def _split_heads(t):
            b, s, _ = t.shape
            return t.reshape(b, s, H, D).transpose(0, 2, 1, 3).reshape(b * H, s, D)
        key = jax.random.key(seed)
        ks = jax.random.split(key, 8)
        x = jax.random.normal(ks[0], (B, S, DIM), dtype=jnp.float32)
        Wq = _xavier(ks[1], (DIM, DIM))
        Wk = _xavier(ks[2], (DIM, DIM))
        Wv = _xavier(ks[3], (DIM, DIM))
        Wo = _xavier(ks[4], (DIM, DIM))
        bq = jax.random.normal(ks[5], (DIM,), dtype=jnp.float32) * 0.02
        bk = jax.random.normal(ks[6], (DIM,), dtype=jnp.float32) * 0.02
        bv = jax.random.normal(ks[7], (DIM,), dtype=jnp.float32) * 0.02
        bo = jnp.zeros((DIM,), dtype=jnp.float32)
        return {'x': x, 'Wq': Wq, 'bq': bq, 'Wk': Wk, 'bk': bk, 'Wv': Wv, 'bv': bv, 'Wo': Wo, 'bo': bo}
    _L0_attn_in = _L0_attn_setup()

    def _L0_ffn_setup():
        import jax, jax.numpy as jnp
        import numpy as np
        D_MODEL = 512
        key = jax.random.key(seed)
        k_x, k_w, k_a1, k_a2 = jax.random.split(key, 4)
        x = jax.random.normal(k_x, (4, 1024, D_MODEL), dtype=jnp.float32)
        weight = jax.random.normal(k_w, (D_MODEL, D_MODEL), dtype=jnp.float32) * 0.02
        aux_weight1 = jax.random.normal(k_a1, (D_MODEL, D_MODEL), dtype=jnp.float32) * 0.02
        aux_weight2 = jax.random.normal(k_a2, (D_MODEL, D_MODEL), dtype=jnp.float32) * 0.02
        bias = jnp.zeros((D_MODEL,), dtype=jnp.float32)
        return {'x': x, 'weight': weight, 'aux_weight1': aux_weight1, 'aux_weight2': aux_weight2, 'bias': bias}
    _L0_ffn_in = _L0_ffn_setup()
    _d = {'L0_attn_x': _L0_attn_in['x'], 'L0_attn_Wq': _L0_attn_in['Wq'], 'L0_attn_bq': _L0_attn_in['bq'], 'L0_attn_Wk': _L0_attn_in['Wk'], 'L0_attn_bk': _L0_attn_in['bk'], 'L0_attn_Wv': _L0_attn_in['Wv'], 'L0_attn_bv': _L0_attn_in['bv'], 'L0_attn_Wo': _L0_attn_in['Wo'], 'L0_attn_bo': _L0_attn_in['bo'], 'L0_ffn_weight': _L0_ffn_in['weight'], 'L0_ffn_aux_weight1': _L0_ffn_in['aux_weight1'], 'L0_ffn_aux_weight2': _L0_ffn_in['aux_weight2'], 'L0_ffn_bias': _L0_ffn_in['bias']}
    _x0 = _d['L0_attn_x']
    _d['L0_attn_x'] = jax.random.normal(jax.random.fold_in(jax.random.key(seed), 1), (8, 2048, 512), dtype=_x0.dtype)
    del _x0
    return _d

def reference(L0_attn_x, L0_attn_Wq, L0_attn_bq, L0_attn_Wk, L0_attn_bk, L0_attn_Wv, L0_attn_bv, L0_attn_Wo, L0_attn_bo, L0_ffn_weight, L0_ffn_aux_weight1, L0_ffn_aux_weight2, L0_ffn_bias):

    def _L0_attn_ref(x, Wq, bq, Wk, bk, Wv, bv, Wo, bo):
        import jax, jax.numpy as jnp
        import numpy as np
        B, S, DIM, H = (2, 1024, 512, 16)
        D = DIM // H

        def _xavier(key, shape):
            a = float(np.sqrt(6.0 / (shape[0] + shape[1])))
            return jax.random.uniform(key, shape, minval=-a, maxval=a, dtype=jnp.float32)

        def _split_heads(t):
            b, s, _ = t.shape
            return t.reshape(b, s, H, D).transpose(0, 2, 1, 3).reshape(b * H, s, D)
        b, s, _ = x.shape
        q = _split_heads(x @ Wq.T + bq)
        k = _split_heads(x @ Wk.T + bk)
        v = _split_heads(x @ Wv.T + bv)
        q = jnp.exp(q)
        k = jnp.exp(k)
        kv = jnp.cumsum(k[:, :, :, None] * v[:, :, None, :], axis=1)
        k1 = jnp.cumsum(k, axis=1)
        num = jnp.einsum('zsD,zsDd->zsd', q, kv)
        den = jnp.sum(q * k1, axis=-1, keepdims=True)
        out = num / den
        out = out.reshape(b, H, s, D).transpose(0, 2, 1, 3).reshape(b, s, DIM)
        return out @ Wo.T + bo

    def _L0_ffn_ref(x, weight, aux_weight1, aux_weight2, bias):
        import jax, jax.numpy as jnp
        import numpy as np
        D_MODEL = 512
        h = jnp.einsum('btc,cd->btd', x, weight)
        h = jnp.einsum('btc,cd->btd', h, aux_weight1)
        h = jnp.einsum('btc,cd->btd', h, aux_weight2)
        return jnp.tanh(h + bias)
    x = L0_attn_x
    x = _layernorm(x + _L0_attn_ref(x, L0_attn_Wq, L0_attn_bq, L0_attn_Wk, L0_attn_bk, L0_attn_Wv, L0_attn_bv, L0_attn_Wo, L0_attn_bo), axis=-1)
    x = _layernorm(x + _L0_ffn_ref(x, L0_ffn_weight, L0_ffn_aux_weight1, L0_ffn_aux_weight2, L0_ffn_bias), axis=-1)
    return x

_drawn_inputs = setup_inputs


def setup_inputs(seed=0):
    import zlib

    import numpy as np

    out = dict(_drawn_inputs(seed))
    spreads = {'L0_attn_bo': (0.0, 0.1), 'L0_ffn_bias': (0.0, 0.1)}
    factors = {'L0_attn_Wq': 3.318, 'L0_attn_bq': 8.0, 'L0_attn_bk': 8.0, 'L0_attn_bv': 2.866}
    for name, (base, spread) in spreads.items():
        noise = np.random.default_rng([zlib.crc32(name.encode()), seed]).standard_normal(out[name].shape)
        drawn = base * np.exp(spread * noise) if base else spread * noise
        out[name] = jnp.asarray(drawn.astype(out[name].dtype))
    for name, factor in factors.items():
        out[name] = (out[name] * factor).astype(out[name].dtype)
    return out
```

```python
import concourse.bass as bass
from concourse import mybir
from contextlib import ExitStack


def linear_attention_ffn_kernel(nc, x, wqT, wkT, wvT, woT, bq, bk, bv, bo, w, a1T, a2, bf, out):
    F32 = mybir.dt.float32
    F32R = mybir.dt.float32r
    ALU = mybir.AluOpType
    ACT = mybir.ActivationFunctionType

    P = 128
    B, S, D = x.shape
    NK = D // P
    HD = 32
    HG = P // HD
    QUAD = 4
    NI = S // P
    NT = NI * B
    EPS = 1e-5
    Q_SHIFT = 8.0
    XIN = 4
    assert B == 2 * QUAD and NI >= 3

    x_t = x.rearrange("b (i p) d -> b i p d", p=P)
    out_t = out.rearrange("b (i p) d -> b i p d", p=P)

    ctx = ExitStack()
    with ctx:
        def sb(name, shape, dt=F32):
            return ctx.enter_context(nc.sbuf_tensor(name, shape, dt))

        def sem(name):
            return ctx.enter_context(nc.semaphore(name))

        WqH, WqL, WkH, WkL, WvH, WvL, WoH, WoL, WfH, WfL = [
            sb(n, [P, NK, D], F32R) for n in
            ("WqH", "WqL", "WkH", "WkL", "WvH", "WvL", "WoH", "WoL", "WfH", "WfL")]
        xin = sb("xin", [P, XIN, D])
        xres = sb("xres", [P, 2, D])
        xTH = sb("xTH", [P, 2, NK, QUAD * P], F32R)
        xTL = sb("xTL", [P, 2, NK, QUAD * P], F32R)
        QT = sb("QT", [P, 2, NK, QUAD * P])
        KT = sb("KT", [P, 2, NK, QUAD * P])
        V = sb("V", [P, 2, D])
        A = sb("A", [P, HG, NK, P])
        Ktok = sb("Ktok", [P, D])
        qk1 = sb("qk1", [P, NK, P])
        o = sb("o", [P, NK, P])
        oH = sb("oH", [P, NK, P], F32R)
        oL = sb("oL", [P, NK, P], F32R)
        r = sb("r", [P, D])
        x1 = sb("x1", [P, 2, D])
        x1H = sb("x1H", [P, NK, P], F32R)
        x1L = sb("x1L", [P, NK, P], F32R)
        z = sb("z", [P, D])
        y = sb("y", [P, 2, D])
        state = sb("state", [P, B, NK, HD])
        k1 = sb("k1", [P, B, NK])
        cbc = sb("cbc", [P, D])
        bfbc = sb("bfbc", [P, D])
        bcol = sb("bcol", [P, 3, NK])
        ident = sb("ident", [P, P])
        blockones = sb("blockones", [P, P])
        ones = sb("ones", [P, P])
        bnst = sb("bnst", [P, 2, 6])
        mv1 = sb("mv1", [P, 2])
        mv2 = sb("mv2", [P, 2])
        ve = sb("ve", [P, 2])
        rstd = sb("rstd", [P, 2])
        mhalf = sb("mhalf", [P, 1])

        SC = ctx.enter_context(nc.psum_tensor("SC", [P, HG, NK * P], F32))
        G = [ctx.enter_context(nc.psum_tensor(f"G{i}", [P, D], F32)) for i in range(4)]
        den_ps, oproj_ps, ktr_ps, qproj_ps = G[0], G[1], G[2], G[3]
        num_ps, x1tr_ps, kproj_ps, state_ps = G[0], G[1], G[2], G[3]
        ffn_ps, v_ps, xtr_ps = G[0], G[1], G[2]

        den_done, scores_done, oproj_done, ktr_done, qproj_done, num_done, x1tr_done, kproj_done, state_done, \
            ffn_done, v_done, xtr_done = [sem(n) for n in (
                "den_done", "scores_done", "oproj_done", "ktr_done", "qproj_done", "num_done", "x1tr_done",
                "kproj_done", "state_done", "ffn_done", "v_done", "xtr_done")]
        scores_out = [sem(f"scores_out{j}") for j in range(HG)]
        ktok_ready, q_ready, k_ready, oh_ready, x1h_ready, tanh_ready, v_ready, xh_ready = [sem(n) for n in (
            "ktok_ready", "q_ready", "k_ready", "oh_ready", "x1h_ready", "tanh_ready", "v_ready", "xh_ready")]
        recip_ready, r_ready, bn1_ready, stats1_ready, x1_ready, o_ready, x1l_ready, state_ready, qk1_ready, \
            z_ready, bn2_ready, stats2_ready, out_ready, xl_ready = [sem(n) for n in (
                "recip_ready", "r_ready", "bn1_ready", "stats1_ready", "x1_ready", "o_ready", "x1l_ready",
                "state_ready", "qk1_ready", "z_ready", "bn2_ready", "stats2_ready", "out_ready", "xl_ready")]
        scan_ready = sem("scan_ready")                
        k1_ready = sem("k1_ready")
        masked = sem("masked")                        
        ve1_ready, rstd1_ready, ve2_ready, rstd2_ready, ol_ready, y_ready, xb_ready = [sem(n) for n in (
            "ve1_ready", "rstd1_ready", "ve2_ready", "rstd2_ready", "ol_ready", "y_ready", "xb_ready")]
        xin_loaded = [sem(f"xin_loaded{i}") for i in range(B)]
        xres_loaded = [sem(f"xres_loaded{i}") for i in range(B)]
        out_stored = [sem(f"out_stored{i}") for i in range(B)]
        small_loaded = sem("small_loaded")
        ffn_w_loaded, wq_loaded, wk_loaded, wv_loaded, wo_loaded = [sem(n) for n in (
            "ffn_w_loaded", "wq_loaded", "wk_loaded", "wv_loaded", "wo_loaded")]
        a12_done, a12_ready, wf_done, c_done = sem("a12_done"), sem("a12_ready"), sem("wf_done"), sem("c_done")
        hi_ready, lo_ready, setup_ready = sem("hi_ready"), sem("lo_ready"), sem("setup_ready")
        ones_zeroed, ident_zeroed, ident_ready, consts_ready, bvrep_ready, bq_ready = [sem(n) for n in (
            "ones_zeroed", "ident_zeroed", "ident_ready", "consts_ready", "bvrep_ready", "bq_ready")]

        a1T_raw, a2_raw = QT[:, 0], QT[:, 1]
        w_raw, wq_raw = KT[:, 0], KT[:, 1]
        wk_raw, wv_raw, wo_raw = QT[:, 0], QT[:, 1], KT[:, 0]
        a12 = A[:, :, :, :].rearrange("p h g q -> p h (g q)")
        bvrep = xres[:, 0, :].rearrange("p (k q) -> p k q", k=NK)

        def wait(engine, semaphore, value):
            if not isinstance(value, int) or value > 0:
                engine.wait_ge(semaphore, value)

        def wait_before(engine, *waits):
            engine.wait_ge(setup_ready, 1)
            for semaphore, value in waits:
                wait(engine, semaphore, value)

        class Chunk:

            def __init__(self, it, engine=None):
                self.it = it
                if engine is not None:
                    self.tiles = {n: engine.compute_val(it * B + n) for n in range(1 - B, 2 * B + 2)}
                    self.loads = {n: engine.compute_val(it * 16 + n * 16) for n in range(0, 3)}

            def count(self, n):
                return min(self.it * B + n, NT) if isinstance(self.it, int) else self.tiles[n]

            def quad_count(self, n):
                return self.count((n // QUAD + 1) * QUAD)

            def dma_count(self, n):
                return (self.it + n // B + 1) * 16 if isinstance(self.it, int) else self.loads[n // B + 1]

            def exists(self, n):
                return not isinstance(self.it, int) or 0 <= B * self.it + n < NT

        def run_slots(engine, slot, ahead, behind):
            for t in range(-ahead, B):
                slot(Chunk(t // B), t % B)
            with engine.Fori(1, NI - 1) as it:
                c = Chunk(it, engine)
                for k in range(B):
                    slot(c, k)
            for t in range(NT - B, NT + behind):
                slot(Chunk(t // B), t % B)

        block = ctx.enter_context(nc.Block())

        @block.sync
        def _(sp):
            def wview(a):
                return a.rearrange("(k p) n -> p k n", p=P)

            sp.dma_start(a1T_raw, wview(a1T)).then_inc(ffn_w_loaded, 16)
            sp.dma_start(a2_raw, wview(a2)).then_inc(ffn_w_loaded, 16)
            sp.dma_start(w_raw, wview(w)).then_inc(ffn_w_loaded, 16)
            sp.dma_start(bcol[:, 0, :], bq).then_inc(small_loaded, 16)
            sp.dma_start(bcol[:, 1, :], bk).then_inc(small_loaded, 16)
            sp.dma_start(bcol[:, 2, :], bv).then_inc(small_loaded, 16)
            sp.dma_start(cbc[:], bo.partition_broadcast(P)).then_inc(small_loaded, 16)
            sp.dma_start(bfbc[:], bf.partition_broadcast(P)).then_inc(small_loaded, 16)
            sp.dma_start(wq_raw, wview(wqT)).then_inc(wq_loaded, 16)
            sp.wait_ge(a12_done, NK)
            sp.dma_start(wk_raw, wview(wkT)).then_inc(wk_loaded, 16)
            sp.dma_start(wv_raw, wview(wvT)).then_inc(wv_loaded, 16)
            sp.wait_ge(wf_done, NK)
            sp.dma_start(wo_raw, wview(woT)).then_inc(wo_loaded, 16)

            def slot(c, k):
                if c.exists(k + 8):
                    wait_before(sp, (xtr_done, c.count(k + 5)))
                    n = k + 8
                    sp.dma_start(xin[:, n % XIN, :], x_t[n % B, c.it + n // B]).then_inc(xin_loaded[n % B], 16)
                if c.exists(k + 1):
                    if isinstance(c.it, int) and c.it * B + k == -1:
                        sp.wait_ge(c_done, 1)
                    wait_before(sp, (r_ready, c.count(k)))
                    n = k + 1
                    sp.dma_start(xres[:, n % 2, :], x_t[n % B, c.it + n // B]).then_inc(xres_loaded[n % B], 16)
                if c.exists(k - 2):
                    wait_before(sp, (out_ready, c.count(k - 1)))
                    n = k - 2
                    sp.dma_start(out_t[n % B, c.it + n // B], y[:, n % 2, :]).then_inc(out_stored[n % B], 16)

            run_slots(sp, slot, 8, 2)
            for n in range(B):
                sp.wait_ge(out_stored[n], 16 * NI)

        @block.tensor
        def _(pe):
            pe.wait_ge(ffn_w_loaded, 48)
            for m in range(NK):
                for k in range(NK):
                    last = nc.tensor.matmul(SC[:, m, :], a1T_raw[:, k, m * P:(m + 1) * P], a2_raw[:, k, :],
                                            start=(k == 0), stop=(k == NK - 1))
                last.then_inc(a12_done, 1)
            for m in range(NK):
                if m == 0:
                    pe.wait_ge(a12_ready, NK)
                for k in range(NK):
                    last = nc.tensor.matmul(G[m][:, :], w_raw[:, k, m * P:(m + 1) * P], a12[:, k, :],
                                            start=(k == 0), stop=(k == NK - 1))
                last.then_inc(wf_done, 1)
            pe.wait_ge(bvrep_ready, NK)
            pe.wait_ge(wo_loaded, 16)
            for k in range(NK):
                last = nc.tensor.matmul(SC[:, 0, :], bvrep[:, k, :], wo_raw[:, k, :],
                                        start=(k == 0), stop=(k == NK - 1))
            last.then_inc(c_done, 1)
            pe.wait_ge(ident_ready, 1)
            pe.wait_ge(consts_ready, 2)
            pe.wait_ge(setup_ready, 1)

            def three_pass(out, statH, statL, movH, movL):
                for k in range(NK):
                    nc.tensor.matmul(out, statH(k), movH(k), start=(k == 0), stop=False)
                    nc.tensor.matmul(out, statH(k), movL(k), start=False, stop=False)
                    last = nc.tensor.matmul(out, statL(k), movH(k), start=False, stop=(k == NK - 1))
                return last

            def slot(c, k):
                b = k % QUAD
                s = (k // QUAD) % 2
                cols = slice(b * P, (b + 1) * P)
                att = c.exists(k)
                ffn = c.exists(k - 1)
                proj = c.exists(k + 4)

                def scores(groups):
                    for g in groups:
                        for j in range(HG):
                            h = slice(j * HD, (j + 1) * HD)
                            last = nc.tensor.matmul(SC[:, j, g * P:(g + 1) * P], KT[h, s, g, cols],
                                                    QT[h, s, g, cols], start=True, stop=True)
                    return last

                if att:
                    wait(pe, qk1_ready, c.count(k + 1))
                    wait(pe, z_ready, c.count(k - 1))
                    nc.tensor.matmul(den_ps[:, :], blockones[:], qk1[:, :, :].rearrange("p g q -> p (g q)"),
                                     start=True, stop=True).then_inc(den_done, 1)
                    wait(pe, k_ready, c.quad_count(k))
                    for j in range(HG):
                        wait(pe, scores_out[j], c.count(k))
                    scores(range(0, NK // 2))
                if ffn:
                    wait(pe, oh_ready, c.count(k))
                    wait(pe, ol_ready, c.count(k))
                    wait(pe, v_ready, c.count(k + 1))
                    three_pass(oproj_ps[:, :], lambda k: oH[:, k, :], lambda k: oL[:, k, :],
                               lambda k: WoH[:, k, :], lambda k: WoL[:, k, :]).then_inc(oproj_done, 1)
                if att:
                    scores(range(NK // 2, NK)).then_inc(scores_done, 1)
                    wait(pe, xl_ready, c.count(k + 8))
                    for g in range(NK):
                        last = nc.tensor.transpose(ktr_ps[:, g * P:(g + 1) * P], KT[:, s, g, cols], ident[:])
                    last.then_inc(ktr_done, 1)
                if proj:
                    ns = 1 - s
                    wait(pe, xl_ready, c.quad_count(k + 4))
                    wait(pe, state_ready, c.count(k))
                    three_pass(qproj_ps[:, :], lambda f: WqH[:, f, b * P:(b + 1) * P],
                               lambda f: WqL[:, f, b * P:(b + 1) * P], lambda f: xTH[:, ns, f, :],
                               lambda f: xTL[:, ns, f, :]).then_inc(qproj_done, 1)
                if att:
                    wait_before(pe, (recip_ready, c.count(k + 1)), (state_ready, c.count(k - 7)))
                    bt = k % B
                    for g in range(NK):
                        for j in range(HG):
                            h = slice(j * HD, (j + 1) * HD)
                            nc.tensor.matmul(num_ps[h, g * P:(g + 1) * P], state[h, bt, g, :], QT[h, s, g, cols],
                                             start=(g == 0), stop=False, skip_group_check=True)
                    wait(pe, v_ready, c.count(k + 1))
                    wait(pe, masked, c.count(k + 1))
                    for g in range(NK):
                        for j in range(HG):
                            h = slice(j * HD, (j + 1) * HD)
                            f0 = g * P + j * HD
                            last = nc.tensor.matmul(num_ps[h, g * P:(g + 1) * P], V[:, k % 2, f0:f0 + HD],
                                                    A[:, j, g, :], start=False, stop=True, skip_group_check=True)
                    last.then_inc(num_done, 1)
                if ffn:
                    wait(pe, x1_ready, c.count(k))
                    wait(pe, r_ready, c.count(k))
                    for g in range(NK):
                        last = nc.tensor.transpose(x1tr_ps[:, g * P:(g + 1) * P],
                                                   x1[:, (k - 1) % 2, g * P:(g + 1) * P], ident[:])
                    last.then_inc(x1tr_done, 1)
                if proj:
                    if att:
                        wait(pe, ktok_ready, c.count(k + 1))
                    else:
                        wait(pe, xl_ready, c.count(k + 8))
                    three_pass(kproj_ps[:, :], lambda f: WkH[:, f, b * P:(b + 1) * P],
                               lambda f: WkL[:, f, b * P:(b + 1) * P], lambda f: xTH[:, ns, f, :],
                               lambda f: xTL[:, ns, f, :]).then_inc(kproj_done, 1)
                if att:
                    wait(pe, ktok_ready, c.count(k + 1))
                    if proj:
                        wait(pe, q_ready, c.count(k + 5))
                    else:
                        wait(pe, state_ready, c.count(k))
                    for g in range(NK):
                        for j in range(HG):
                            f0 = g * P + j * HD
                            last = nc.tensor.matmul(state_ps[j * HD:(j + 1) * HD, g * HD:(g + 1) * HD],
                                                    Ktok[:, f0:f0 + HD], V[:, k % 2, f0:f0 + HD],
                                                    start=True, stop=True)
                    last.then_inc(state_done, 1)
                if ffn:
                    wait(pe, x1h_ready, c.count(k))
                    wait(pe, x1l_ready, c.count(k))
                    wait(pe, o_ready, c.count(k + 1))
                    three_pass(ffn_ps[:, :], lambda f: x1H[:, f, :], lambda f: x1L[:, f, :],
                               lambda f: WfH[:, f, :], lambda f: WfL[:, f, :]).then_inc(ffn_done, 1)
                if c.exists(k + 1):
                    n = k + 1
                    ncols = slice(n % QUAD * P, (n % QUAD + 1) * P)
                    vs = (n // QUAD) % 2
                    wait(pe, x1l_ready, c.count(k))
                    three_pass(v_ps[:, :], lambda f: xTH[:, vs, f, ncols], lambda f: xTL[:, vs, f, ncols],
                               lambda f: WvH[:, f, :], lambda f: WvL[:, f, :]).then_inc(v_done, 1)
                if c.exists(k + 8):
                    n = k + 8
                    wait(pe, xin_loaded[n % B], c.dma_count(n))
                    wait(pe, xl_ready, c.count(k + 8))
                    if proj:
                        wait(pe, k_ready, c.count(k + 5))
                    for g in range(NK):
                        last = nc.tensor.transpose(xtr_ps[:, g * P:(g + 1) * P],
                                                   xin[:, n % XIN, g * P:(g + 1) * P], ident[:])
                    last.then_inc(xtr_done, 1)

            run_slots(pe, slot, 8, 1)

        @block.scalar
        def _(act):
            for m in range(NK):
                act.wait_ge(a12_done, m + 1)
                nc.scalar.activation(a12[:, m, :], SC[:, m, :], ACT.Copy).then_inc(a12_ready, 1)
            for m in range(NK):
                act.wait_ge(wf_done, m + 1)
                nc.scalar.activation(WfH[:, m, :], G[m][:, :], ACT.Copy).then_inc(hi_ready, 1)
            for loaded, hi, raw in ((wq_loaded, WqH, wq_raw), (wk_loaded, WkH, wk_raw),
                                    (wv_loaded, WvH, wv_raw), (wo_loaded, WoH, wo_raw)):
                act.wait_ge(loaded, 16)
                nc.scalar.activation(hi[:, :, :], raw, ACT.Copy).then_inc(hi_ready, 1)
            act.wait_ge(small_loaded, 80)
            act.wait_ge(bq_ready, 1)
            act.wait_ge(setup_ready, 1)

            def slot(c, k):
                b = k % QUAD
                ns = 1 - (k // QUAD) % 2
                att = c.exists(k)
                ffn = c.exists(k - 1)
                proj = c.exists(k + 4)
                if att:
                    wait(act, scores_done, c.count(k + 1))
                    wait(act, num_done, c.count(k))
                    for j in range(HG):
                        nc.scalar.activation(A[:, j, :, :].rearrange("p g q -> p (g q)"), SC[:, j, :],
                                             ACT.Copy).then_inc(scores_out[j], 1)
                    wait(act, ktr_done, c.count(k + 1))
                    wait(act, state_done, c.count(k))
                    nc.scalar.activation(Ktok[:, :], ktr_ps[:, :], ACT.Copy).then_inc(ktok_ready, 1)
                if proj:
                    wait(act, qproj_done, c.count(k + 5))
                    wait(act, num_done, c.quad_count(k - 4))
                    nc.scalar.activation(QT[:, ns, b, :], qproj_ps[:, :], ACT.Exp,
                                         bias=bcol[:, 0, b:b + 1]).then_inc(q_ready, 1)
                if ffn:
                    wait(act, x1tr_done, c.count(k))
                    wait(act, ffn_done, c.count(k - 1))
                    nc.scalar.activation(x1H[:, :, :].rearrange("p g q -> p (g q)"), x1tr_ps[:, :],
                                         ACT.Copy).then_inc(x1h_ready, 1)
                if att:
                    wait(act, o_ready, c.count(k + 1))
                    wait(act, oproj_done, c.count(k))
                    nc.scalar.activation(oH[:, :, :], o[:, :, :], ACT.Copy).then_inc(oh_ready, 1)
                if proj:
                    wait(act, kproj_done, c.count(k + 5))
                    wait(act, num_done, c.quad_count(k - 4))
                    nc.scalar.activation(KT[:, ns, b, :], kproj_ps[:, :], ACT.Exp,
                                         bias=bcol[:, 1, b:b + 1]).then_inc(k_ready, 1)
                if ffn:
                    wait(act, z_ready, c.count(k))
                    nc.scalar.activation(z[:, :], z[:, :], ACT.Tanh).then_inc(tanh_ready, 1)
                if c.exists(k + 1):
                    wait(act, v_done, c.count(k + 2))
                    wait(act, state_done, c.count(k))
                    nc.scalar.activation(V[:, (k + 1) % 2, :], v_ps[:, :], ACT.Copy).then_inc(v_ready, 1)
                if c.exists(k + 8):
                    wait(act, xtr_done, c.count(k + 9))
                    nc.scalar.activation(xTH[:, (k // QUAD) % 2, :, b * P:(b + 1) * P],
                                         xtr_ps[:, :].rearrange("p (g q) -> p g q", g=NK),
                                         ACT.Copy).then_inc(xh_ready, 1)

            run_slots(act, slot, 8, 1)

        @block.vector
        def _(dve):
            for n in range(HG):
                nc.vector.memset(blockones[n * HD:(n + 1) * HD, :], 0.0).then_inc(ones_zeroed, 1)
            dve.wait_ge(ones_zeroed, HG)
            for n in range(HG):
                last = nc.vector.memset(blockones[n * HD:(n + 1) * HD, n * HD:(n + 1) * HD], 1.0)
            last.then_inc(consts_ready, 1)
            nc.vector.memset(state[:, :, :, :], 0.0)
            nc.vector.memset(k1[:, :, :], 0.0)
            nc.vector.memset(ones[:], 1.0)
            nc.vector.memset(bvrep, 1.0).then_inc(consts_ready, 1)
            dve.wait_ge(consts_ready, 2)
            dve.wait_ge(small_loaded, 80)
            nc.vector.tensor_scalar(bcol[:, 0, :], bcol[:, 0, :], -Q_SHIFT, None, ALU.add).then_inc(bq_ready, 1)
            for c in range(NK):
                nc.vector.tensor_scalar(bvrep[:, c, :], bvrep[:, c, :], bcol[:, 2, c:c + 1], None,
                                        ALU.mult).then_inc(bvrep_ready, 1)
            for m in range(NK):
                dve.wait_ge(hi_ready, m + 1)
                nc.vector.tensor_tensor(WfL[:, m, :], G[m][:, :], WfH[:, m, :].bitcast(F32),
                                        ALU.subtract).then_inc(lo_ready, 1)
            for n, (lo, hi, raw) in enumerate(((WqL, WqH, wq_raw), (WkL, WkH, wk_raw), (WvL, WvH, wv_raw),
                                               (WoL, WoH, wo_raw))):
                dve.wait_ge(hi_ready, NK + n + 1)
                nc.vector.tensor_tensor(lo[:, :, :], raw, hi[:, :, :].bitcast(F32),
                                        ALU.subtract).then_inc(lo_ready, 1)
            dve.wait_ge(c_done, 1)
            dve.wait_ge(lo_ready, NK + 4)
            nc.vector.tensor_tensor(cbc[:, :], cbc[:, :], SC[:, 0, :], ALU.add).then_inc(setup_ready, 1)

            def slot(c, k):
                b = k % QUAD
                bt = k % B
                if c.exists(k):
                    wait(dve, den_done, c.count(k + 1))
                    wait(dve, oh_ready, c.count(k))
                    wait(dve, ol_ready, c.count(k))
                    nc.vector.reciprocal(o[:, :, :].rearrange("p g q -> p (g q)"),
                                         den_ps[:, :]).then_inc(recip_ready, 1)
                if c.exists(k - 2):
                    wait(dve, y_ready, c.count(k - 1))
                    nc.vector.bn_stats(bnst[:, 1, :], y[:, k % 2, :]).then_inc(bn2_ready, 1)
                    wait_before(dve, (bn2_ready, c.count(k - 1)), (rstd2_ready, c.count(k - 2)))
                    nc.vector.bn_aggr(mv2[:, :], bnst[:, 1, :]).then_inc(stats2_ready, 1)
                if c.exists(k - 1):
                    wait(dve, oproj_done, c.count(k))
                    wait(dve, xb_ready, c.count(k))
                    wait(dve, x1_ready, c.count(k - 1))
                    nc.vector.tensor_tensor(r[:, :], oproj_ps[:, :], xres[:, (k - 1) % 2, :],
                                            ALU.add).then_inc(r_ready, 1)
                    wait(dve, r_ready, c.count(k))
                    nc.vector.bn_stats(bnst[:, 0, :], r[:, :]).then_inc(bn1_ready, 1)
                    wait_before(dve, (bn1_ready, c.count(k)))
                    nc.vector.bn_aggr(mv1[:, :], bnst[:, 0, :]).then_inc(stats1_ready, 1)
                if c.exists(k - 2):
                    wait(dve, rstd2_ready, c.count(k - 1))
                    wait(dve, stats2_ready, c.count(k - 1))
                    nc.vector.tensor_scalar(y[:, k % 2, :], y[:, k % 2, :], mv2[:, 0:1], rstd[:, 1:2],
                                            ALU.subtract, ALU.mult).then_inc(out_ready, 1)
                if c.exists(k - 1):
                    wait(dve, rstd1_ready, c.count(k))
                    wait(dve, y_ready, c.count(k - 2))
                    nc.vector.tensor_scalar(x1[:, (k - 1) % 2, :], r[:, :], mv1[:, 0:1], rstd[:, 0:1],
                                            ALU.subtract, ALU.mult).then_inc(x1_ready, 1)
                if c.exists(k):
                    wait(dve, num_done, c.count(k + 1))
                    wait(dve, recip_ready, c.count(k + 1))
                    oflat = o[:, :, :].rearrange("p g q -> p (g q)")
                    nc.vector.tensor_tensor(oflat, num_ps[:, :], oflat, ALU.mult).then_inc(o_ready, 1)
                if c.exists(k - 1):
                    wait(dve, x1h_ready, c.count(k))
                    nc.vector.tensor_tensor(x1L[:, :, :].rearrange("p g q -> p (g q)"), x1tr_ps[:, :],
                                            x1H[:, :, :].rearrange("p g q -> p (g q)").bitcast(F32),
                                            ALU.subtract).then_inc(x1l_ready, 1)
                if c.exists(k):
                    wait(dve, state_done, c.count(k + 1))
                    sflat = state[:, bt, :, :].rearrange("p g d -> p (g d)")
                    nc.vector.tensor_tensor(sflat, state_ps[:, 0:NK * HD], sflat, ALU.add).then_inc(state_ready, 1)
                if c.exists(k + 1):
                    n = k + 1
                    nb, nq = n % B, (n // QUAD) % 2
                    ncols = slice(n % QUAD * P, (n % QUAD + 1) * P)
                    wait(dve, k_ready, c.quad_count(n))
                    wait(dve, den_done, c.count(k + 1))
                    wait(dve, k1_ready, c.count(k - 6))
                    for g in range(NK):
                        last = nc.vector.tensor_tensor_scan(qk1[:, g, :], ones[:], KT[:, nq, g, ncols],
                                                            k1[:, nb, g:g + 1], ALU.mult, ALU.add)
                    last.then_inc(scan_ready, 1)
                    wait(dve, scan_ready, c.count(k + 2))
                    nc.vector.tensor_copy(k1[:, nb, :], qk1[:, :, P - 1]).then_inc(k1_ready, 1)
                    wait(dve, k1_ready, c.count(k + 2))
                    nc.vector.tensor_tensor(qk1[:, :, :], qk1[:, :, :], QT[:, nq, :, ncols],
                                            ALU.mult).then_inc(qk1_ready, 1)
                if c.exists(k - 1):
                    wait(dve, ffn_done, c.count(k))
                    wait(dve, y_ready, c.count(k - 1))
                    nc.vector.tensor_tensor(z[:, :], ffn_ps[:, :], bfbc[:, :], ALU.add).then_inc(z_ready, 1)
                if c.exists(k + 8):
                    xs = (k // QUAD) % 2
                    wait(dve, xh_ready, c.count(k + 9))
                    nc.vector.tensor_tensor(xTL[:, xs, :, b * P:(b + 1) * P],
                                            xtr_ps[:, :].rearrange("p (g q) -> p g q", g=NK),
                                            xTH[:, xs, :, b * P:(b + 1) * P].bitcast(F32),
                                            ALU.subtract).then_inc(xl_ready, 1)

            run_slots(dve, slot, 8, 2)

        @block.gpsimd
        def _(pool):
            nc.gpsimd.memset(mhalf[:], -0.5)
            nc.gpsimd.memset(ident[:], 0.0).then_inc(ident_zeroed, 1)
            pool.wait_ge(ident_zeroed, 1)
            nc.gpsimd.affine_select(out=ident[:], in_=ident[:], compare_op=ALU.not_equal, fill=1.0, base=0,
                                    pattern=[[-1, P]], channel_multiplier=1).then_inc(ident_ready, 1)
            pool.wait_ge(ident_ready, 1)
            pool.wait_ge(setup_ready, 1)

            def slot(c, k):
                if c.exists(k - 2):
                    wait_before(pool, (stats2_ready, c.count(k - 1)))
                    nc.gpsimd.tensor_scalar(ve[:, 1:2], mv2[:, 1:2], EPS, None, ALU.add).then_inc(ve2_ready, 1)
                    wait(pool, ve2_ready, c.count(k - 1))
                    wait(pool, out_ready, c.count(k - 2))
                    nc.gpsimd.tensor_tensor(rstd[:, 1:2], ve[:, 1:2], mhalf[:, :], ALU.pow).then_inc(rstd2_ready, 1)
                if c.exists(k - 1):
                    wait_before(pool, (stats1_ready, c.count(k)))
                    nc.gpsimd.tensor_scalar(ve[:, 0:1], mv1[:, 1:2], EPS, None, ALU.add).then_inc(ve1_ready, 1)
                    wait(pool, ve1_ready, c.count(k))
                    wait(pool, x1_ready, c.count(k - 1))
                    nc.gpsimd.tensor_tensor(rstd[:, 0:1], ve[:, 0:1], mhalf[:, :], ALU.pow).then_inc(rstd1_ready, 1)
                if c.exists(k):
                    for j in range(HG):
                        wait_before(pool, (scores_out[j], c.count(k + 1)))
                        last = nc.gpsimd.affine_select(out=A[:, j, :, :], in_=A[:, j, :, :], compare_op=ALU.is_ge,
                                                fill=0.0, base=0, pattern=[[0, NK], [1, P]],
                                                channel_multiplier=-1)
                    last.then_inc(masked, 1)
                    wait(pool, oh_ready, c.count(k + 1))
                    wait(pool, oproj_done, c.count(k))
                    nc.gpsimd.tensor_tensor(oL[:, :, :], o[:, :, :], oH[:, :, :].bitcast(F32),
                                            ALU.subtract).then_inc(ol_ready, 1)
                if c.exists(k - 1):
                    wait(pool, tanh_ready, c.count(k))
                    n = k - 1
                    wait(pool, out_stored[(k - 3) % B], c.dma_count(k - 3))
                    nc.gpsimd.tensor_tensor(y[:, n % 2, :], z[:, :], x1[:, n % 2, :], ALU.add).then_inc(y_ready, 1)
                if c.exists(k):
                    wait(pool, xres_loaded[k], c.dma_count(k))
                    nc.gpsimd.tensor_tensor(xres[:, k % 2, :], xres[:, k % 2, :], cbc[:, :],
                                            ALU.add).then_inc(xb_ready, 1)

            run_slots(pool, slot, 0, 2)


def kernel(**inputs):
    import numpy as np
    import concourse.bacc as bacc
    from concourse.bass_utils import run_bass_kernel_spmd

    def by_partition(v):
        return np.ascontiguousarray(np.asarray(v).reshape(-1, 128).T)

    def transposed(m):
        return np.ascontiguousarray(np.asarray(m).T)

    arrays = {
        "x": np.ascontiguousarray(inputs["L0_attn_x"]),
        "wqT": transposed(inputs["L0_attn_Wq"]),
        "wkT": transposed(inputs["L0_attn_Wk"]),
        "wvT": transposed(inputs["L0_attn_Wv"]),
        "woT": transposed(inputs["L0_attn_Wo"]),
        "bq": by_partition(inputs["L0_attn_bq"]),
        "bk": by_partition(inputs["L0_attn_bk"]),
        "bv": by_partition(inputs["L0_attn_bv"]),
        "bo": np.ascontiguousarray(inputs["L0_attn_bo"]),
        "wT": transposed(inputs["L0_ffn_weight"]),
        "a1T": transposed(inputs["L0_ffn_aux_weight1"]),
        "a2": np.ascontiguousarray(inputs["L0_ffn_aux_weight2"]),
        "bf": np.ascontiguousarray(inputs["L0_ffn_bias"]),
    }
    nc = bacc.Bacc("TRN2", target_bir_lowering=False, num_devices=1)
    aps = [nc.dram_tensor(n, a.shape, mybir.dt.from_np(a.dtype), kind="ExternalInput").ap()
           for n, a in arrays.items()]
    out = nc.dram_tensor("out", arrays["x"].shape, mybir.dt.float32, kind="ExternalOutput").ap()
    linear_attention_ffn_kernel(nc, *aps, out)
    result = run_bass_kernel_spmd(nc, [arrays], core_ids=[0])
    return result.results[0]["out"]
```

```python
import concourse.bass as bass
from concourse import mybir
from contextlib import ExitStack


def linear_attention_ffn_kernel(nc, x, wqT, wkT, wvT, woT, bq, bk, bv, bo, w, a1T, a2, bf, out):
    F32 = mybir.dt.float32
    F32R = mybir.dt.float32r
    ALU = mybir.AluOpType
    ACT = mybir.ActivationFunctionType

    P = 128
    B, S, D = x.shape
    NK = D // P
    HD = 32
    HG = P // HD
    QUAD = 4
    NI = S // P
    NT = NI * B
    EPS = 1e-5
    Q_SHIFT = 8.0
    XIN = 2
    assert B == 2 * QUAD and NI >= 3

    x_t = x.rearrange("b (i p) d -> b i p d", p=P)
    out_t = out.rearrange("b (i p) d -> b i p d", p=P)

    ctx = ExitStack()
    with ctx:
        def sb(name, shape, dt=F32):
            return ctx.enter_context(nc.sbuf_tensor(name, shape, dt))

        def sem(name):
            return ctx.enter_context(nc.semaphore(name))

        WqH, WqL, WkH, WkL, WvH, WvL, WoH, WoL, WfH, WfL = [
            sb(n, [P, NK, D], F32R) for n in
            ("WqH", "WqL", "WkH", "WkL", "WvH", "WvL", "WoH", "WoL", "WfH", "WfL")]
        xin = sb("xin", [P, XIN, D])
        xres = sb("xres", [P, 2, D])
        xTH = sb("xTH", [P, 2, NK, QUAD * P], F32R)
        xTL = sb("xTL", [P, 2, NK, QUAD * P], F32R)
        QT = sb("QT", [P, 2, NK, QUAD * P])
        KT = sb("KT", [P, 2, NK, QUAD * P])
        V = sb("V", [P, 2, D])
        A = sb("A", [P, HG, NK, P])
        WK = sb("WK", [P, 8, D])
        r = WK[:, 0, :]
        z = WK[:, 1, :]
        y = WK[:, 2:4, :]
        x1 = WK[:, 4:6, :]
        Ktok = WK[:, 6, :]
        qk1 = WK[:, 7, :].rearrange("p (g q) -> p g q", g=NK)
        qk1H = sb("qk1H", [P, D], F32R)
        qk1L = sb("qk1L", [P, D], F32R)
        o = sb("o", [P, NK, P])
        oH = sb("oH", [P, NK, P], F32R)
        oL = sb("oL", [P, NK, P], F32R)
        x1H = sb("x1H", [P, NK, P], F32R)
        x1L = sb("x1L", [P, NK, P], F32R)
        state = sb("state", [P, B, NK, HD])
        stateB = sb("stateB", [P, NK, P])
        k1 = sb("k1", [P, B, NK])
        cbc = sb("cbc", [P, D])
        bfbc = sb("bfbc", [P, D])
        bcol = sb("bcol", [P, 3, NK])
        ident = sb("ident", [P, P])
        blockones = sb("blockones", [P, P])
        blockonesR = sb("blockonesR", [P, P], F32R)
        ones = sb("ones", [P, 1])
        bnst = sb("bnst", [P, 2, 6])
        mv1 = sb("mv1", [P, 2])
        mv2 = sb("mv2", [P, 2])
        ve = sb("ve", [P, 2])
        rstd = sb("rstd", [P, 2])
        mhalf = sb("mhalf", [P, 1])

        SC = ctx.enter_context(nc.psum_tensor("SC", [P, HG, NK * P], F32))
        G = [ctx.enter_context(nc.psum_tensor(f"G{i}", [P, D], F32)) for i in range(4)]
        den_ps, oproj_ps, ktr_ps, qproj_ps = G[0], G[1], G[2], G[3]
        num_ps, x1tr_ps, kproj_ps, state_ps = G[0], G[1], G[2], G[3]
        ffn_ps, v_ps, xtr_ps = G[0], G[1], G[2]

        den_done, scores_done, oproj_done, ktr_done, qproj_done, num_done, x1tr_done, kproj_done, state_done, \
            ffn_done, v_done, xtr_done = [sem(n) for n in (
                "den_done", "scores_done", "oproj_done", "ktr_done", "qproj_done", "num_done", "x1tr_done",
                "kproj_done", "state_done", "ffn_done", "v_done", "xtr_done")]
        scores_out = [sem(f"scores_out{j}") for j in range(HG)]
        ktok_ready, q_ready, k_ready, oh_ready, x1h_ready, tanh_ready, v_ready, xh_ready, qk1h_ready, \
            stateb_ready = [sem(n) for n in (
                "ktok_ready", "q_ready", "k_ready", "oh_ready", "x1h_ready", "tanh_ready", "v_ready", "xh_ready",
                "qk1h_ready", "stateb_ready")]
        recip_ready, r_ready, bn1_ready, stats1_ready, x1_ready, o_ready, x1l_ready, state_ready, qk1_ready, \
            z_ready, bn2_ready, stats2_ready, out_ready, xl_ready = [sem(n) for n in (
                "recip_ready", "r_ready", "bn1_ready", "stats1_ready", "x1_ready", "o_ready", "x1l_ready",
                "state_ready", "qk1_ready", "z_ready", "bn2_ready", "stats2_ready", "out_ready", "xl_ready")]
        scan_ready = sem("scan_ready")                
        k1_ready = sem("k1_ready")
        masked = sem("masked")                        
        ve1_ready, rstd1_ready, ve2_ready, rstd2_ready, ol_ready, y_ready, xb_ready, \
            qk1l_ready = [sem(n) for n in (
            "ve1_ready", "rstd1_ready", "ve2_ready", "rstd2_ready", "ol_ready", "y_ready", "xb_ready",
                "qk1l_ready")]
        xin_loaded = [sem(f"xin_loaded{i}") for i in range(B)]
        xres_loaded = [sem(f"xres_loaded{i}") for i in range(B)]
        out_stored = [sem(f"out_stored{i}") for i in range(B)]
        small_loaded = sem("small_loaded")
        ffn_w_loaded, wq_loaded, wk_loaded, wv_loaded, wo_loaded = [sem(n) for n in (
            "ffn_w_loaded", "wq_loaded", "wk_loaded", "wv_loaded", "wo_loaded")]
        a12_done, a12_ready, wf_done, c_done = sem("a12_done"), sem("a12_ready"), sem("wf_done"), sem("c_done")
        wfh_ready, wfl_ready, c_ready = sem("wfh_ready"), sem("wfl_ready"), sem("c_ready")
        wqh_ready, wkh_ready, wvh_ready, woh_ready, wql_ready, wkl_ready, wvl_ready, wol_ready = [sem(n) for n in (
            "wqh_ready", "wkh_ready", "wvh_ready", "woh_ready", "wql_ready", "wkl_ready", "wvl_ready", "wol_ready")]
        biases_loaded = sem("biases_loaded")
        ones_zeroed, ident_zeroed, ident_ready, consts_ready, bvrep_ready, bq_ready = [sem(n) for n in (
            "ones_zeroed", "ident_zeroed", "ident_ready", "consts_ready", "bvrep_ready", "bq_ready")]

        wq_raw, wk_raw, a2_raw, w_raw = QT[:, 1], KT[:, 1], WK[:, 0:4, :], WK[:, 4:8, :]
        a1T_raw = A[:, :, :, :].rearrange("p h g q -> p h (g q)")
        a12, wv_raw, wo_raw = wq_raw, wk_raw, a1T_raw
        bvrep = xres[:, 0, :].rearrange("p (k q) -> p k q", k=NK)

        def wait(engine, semaphore, value):
            if not isinstance(value, int) or value > 0:
                engine.wait_ge(semaphore, value)

        def wait_before(engine, *waits):
            engine.wait_ge(ident_ready, 1)
            for semaphore, value in waits:
                wait(engine, semaphore, value)

        class Chunk:

            def __init__(self, it, engine=None):
                self.it = it
                if engine is not None:
                    self.tiles = {n: engine.compute_val(it * B + n) for n in range(1 - B, 2 * B + 2)}
                    self.loads = {n: engine.compute_val(it * 16 + n * 16) for n in range(0, 3)}

            def count(self, n):
                return min(self.it * B + n, NT) if isinstance(self.it, int) else self.tiles[n]

            def quad_count(self, n):
                return self.count((n // QUAD + 1) * QUAD)

            def dma_count(self, n):
                return (self.it + n // B + 1) * 16 if isinstance(self.it, int) else self.loads[n // B + 1]

            def exists(self, n):
                return not isinstance(self.it, int) or 0 <= B * self.it + n < NT

        def run_slots(engine, slot, ahead, behind, setup={}):
            for t in range(-ahead, B):
                slot(Chunk(t // B), t % B)
                if t in setup:
                    setup[t]()
            with engine.Fori(1, NI - 1) as it:
                c = Chunk(it, engine)
                for k in range(B):
                    slot(c, k)
            for t in range(NT - B, NT + behind):
                slot(Chunk(t // B), t % B)

        block = ctx.enter_context(nc.Block())

        @block.sync
        def _(sp):
            def wview(a):
                return a.rearrange("(k p) n -> p k n", p=P)

            def load_first_weights():
                sp.dma_start(bcol[:, 0, :], bq).then_inc(biases_loaded, 16)
                sp.dma_start(bcol[:, 1, :], bk).then_inc(biases_loaded, 16)
                sp.dma_start(bcol[:, 2, :], bv).then_inc(biases_loaded, 16)
                sp.dma_start(wq_raw, wview(wqT)).then_inc(wq_loaded, 16)
                sp.dma_start(wk_raw, wview(wkT)).then_inc(wk_loaded, 16)

            def load_ffn_weights():
                sp.dma_start(a1T_raw, wview(a1T)).then_inc(ffn_w_loaded, 16)
                sp.dma_start(a2_raw, wview(a2)).then_inc(ffn_w_loaded, 16)
                sp.dma_start(w_raw, wview(w)).then_inc(ffn_w_loaded, 16)
                sp.dma_start(cbc[:], bo.partition_broadcast(P)).then_inc(small_loaded, 16)
                sp.dma_start(bfbc[:], bf.partition_broadcast(P)).then_inc(small_loaded, 16)

            def load_wv():
                sp.wait_ge(wkl_ready, 1)
                sp.dma_start(wv_raw, wview(wvT)).then_inc(wv_loaded, 16)

            def load_wo():
                sp.wait_ge(a12_done, NK)
                sp.dma_start(wo_raw, wview(woT)).then_inc(wo_loaded, 16)

            def slot(c, k):
                if c.exists(k + 8):
                    wait_before(sp, (xtr_done, c.count(k + 7)))
                    n = k + 8
                    sp.dma_start(xin[:, n % XIN, :], x_t[n % B, c.it + n // B]).then_inc(xin_loaded[n % B], 16)
                if c.exists(k + 1):
                    if isinstance(c.it, int) and c.it * B + k == -1:
                        sp.wait_ge(c_done, 1)
                    wait_before(sp, (r_ready, c.count(k)))
                    n = k + 1
                    sp.dma_start(xres[:, n % 2, :], x_t[n % B, c.it + n // B]).then_inc(xres_loaded[n % B], 16)
                if c.exists(k - 2):
                    wait_before(sp, (out_ready, c.count(k - 1)))
                    n = k - 2
                    sp.dma_start(out_t[n % B, c.it + n // B], y[:, n % 2, :]).then_inc(out_stored[n % B], 16)

            run_slots(sp, slot, 8, 2, {-7: load_first_weights, -5: load_ffn_weights, -4: load_wv,
                                        -2: load_wo})
            for n in range(B):
                sp.wait_ge(out_stored[n], 16 * NI)

        @block.tensor
        def _(pe):
            def multiply_aux():
                pe.wait_ge(ffn_w_loaded, 48)
                for m in range(NK):
                    for k in range(NK):
                        last = nc.tensor.matmul(SC[:, m, :], a1T_raw[:, k, m * P:(m + 1) * P], a2_raw[:, k, :],
                                                start=(k == 0), stop=(k == NK - 1))
                    last.then_inc(a12_done, 1)

            def multiply_weight():
                pe.wait_ge(a12_ready, NK)
                for m in range(NK):
                    for k in range(NK):
                        last = nc.tensor.matmul(SC[:, m, :], w_raw[:, k, m * P:(m + 1) * P], a12[:, k, :],
                                                start=(k == 0), stop=(k == NK - 1))
                    last.then_inc(wf_done, 1)

            def multiply_bv():
                pe.wait_ge(bvrep_ready, NK)
                pe.wait_ge(wo_loaded, 16)
                pe.wait_ge(wfl_ready, NK)
                for k in range(NK):
                    last = nc.tensor.matmul(SC[:, 0, :], bvrep[:, k, :], wo_raw[:, k, :],
                                            start=(k == 0), stop=(k == NK - 1))
                last.then_inc(c_done, 1)
                pe.wait_ge(c_ready, 1)
                pe.wait_ge(consts_ready, 2)

            pe.wait_ge(ident_ready, 1)

            def three_pass(out, statH, statL, movH, movL):
                for k in range(NK):
                    nc.tensor.matmul(out, statH(k), movH(k), start=(k == 0), stop=False)
                    nc.tensor.matmul(out, statH(k), movL(k), start=False, stop=False)
                    last = nc.tensor.matmul(out, statL(k), movH(k), start=False, stop=(k == NK - 1))
                return last

            def slot(c, k):
                b = k % QUAD
                s = (k // QUAD) % 2
                cols = slice(b * P, (b + 1) * P)
                att = c.exists(k)
                ffn = c.exists(k - 1)
                proj = c.exists(k + 4)

                def scores(groups):
                    for g in groups:
                        for j in range(HG):
                            h = slice(j * HD, (j + 1) * HD)
                            last = nc.tensor.matmul(SC[:, j, g * P:(g + 1) * P], KT[h, s, g, cols],
                                                    QT[h, s, g, cols], start=True, stop=True)
                    return last

                if att:
                    wait(pe, qk1h_ready, c.count(k + 1))
                    wait(pe, qk1l_ready, c.count(k + 1))
                    wait(pe, z_ready, c.count(k - 1))
                    nc.tensor.matmul(den_ps[:, :], blockonesR[:], qk1H[:, :], start=True, stop=False)
                    nc.tensor.matmul(den_ps[:, :], blockonesR[:], qk1L[:, :], start=False,
                                     stop=True).then_inc(den_done, 1)
                    wait(pe, k_ready, c.quad_count(k))
                    for j in range(HG):
                        wait(pe, scores_out[j], c.count(k))
                    scores(range(0, NK // 2))
                if ffn:
                    if c.exists(k - 1) and not c.exists(k - 2):
                        pe.wait_ge(woh_ready, 1)
                        pe.wait_ge(wol_ready, 1)
                    wait(pe, oh_ready, c.count(k))
                    wait(pe, ol_ready, c.count(k))
                    wait(pe, v_ready, c.count(k + 1))
                    three_pass(oproj_ps[:, :], lambda k: oH[:, k, :], lambda k: oL[:, k, :],
                               lambda k: WoH[:, k, :], lambda k: WoL[:, k, :]).then_inc(oproj_done, 1)
                if att:
                    scores(range(NK // 2, NK)).then_inc(scores_done, 1)
                    wait(pe, xl_ready, c.count(k + 8))
                    for g in range(NK):
                        last = nc.tensor.transpose(ktr_ps[:, g * P:(g + 1) * P], KT[:, s, g, cols], ident[:])
                    last.then_inc(ktr_done, 1)
                if proj:
                    ns = 1 - s
                    if not c.exists(k + 3):
                        pe.wait_ge(wqh_ready, 1)
                        pe.wait_ge(wql_ready, 1)
                        pe.wait_ge(wkh_ready, 1)
                        pe.wait_ge(wkl_ready, 1)
                    wait(pe, xl_ready, c.quad_count(k + 4))
                    wait(pe, state_ready, c.count(k))
                    three_pass(qproj_ps[:, :], lambda f: WqH[:, f, b * P:(b + 1) * P],
                               lambda f: WqL[:, f, b * P:(b + 1) * P], lambda f: xTH[:, ns, f, :],
                               lambda f: xTL[:, ns, f, :]).then_inc(qproj_done, 1)
                if att:
                    wait(pe, recip_ready, c.count(k + 1))
                    wait(pe, stateb_ready, c.count(k + 1))
                    for g in range(NK):
                        nc.tensor.matmul(num_ps[:, g * P:(g + 1) * P], stateB[:, g, :], QT[:, s, g, cols],
                                         start=(g == 0), stop=False, skip_group_check=True)
                if ffn:
                    wait(pe, x1_ready, c.count(k))
                    wait(pe, r_ready, c.count(k))
                    for g in range(NK):
                        last = nc.tensor.transpose(x1tr_ps[:, g * P:(g + 1) * P],
                                                   x1[:, (k - 1) % 2, g * P:(g + 1) * P], ident[:])
                    last.then_inc(x1tr_done, 1)
                if att:
                    wait(pe, v_ready, c.count(k + 1))
                    wait(pe, masked, c.count(k + 1))
                    for g in range(NK):
                        for j in range(HG):
                            h = slice(j * HD, (j + 1) * HD)
                            f0 = g * P + j * HD
                            last = nc.tensor.matmul(num_ps[h, g * P:(g + 1) * P], V[:, k % 2, f0:f0 + HD],
                                                    A[:, j, g, :], start=False, stop=True, skip_group_check=True)
                    last.then_inc(num_done, 1)
                if proj:
                    if att:
                        wait(pe, ktok_ready, c.count(k + 1))
                    else:
                        wait(pe, xl_ready, c.count(k + 8))
                    three_pass(kproj_ps[:, :], lambda f: WkH[:, f, b * P:(b + 1) * P],
                               lambda f: WkL[:, f, b * P:(b + 1) * P], lambda f: xTH[:, ns, f, :],
                               lambda f: xTL[:, ns, f, :]).then_inc(kproj_done, 1)
                if att:
                    wait(pe, ktok_ready, c.count(k + 1))
                    if proj:
                        wait(pe, q_ready, c.count(k + 5))
                    else:
                        wait(pe, state_ready, c.count(k))
                    for g in range(NK):
                        for j in range(HG):
                            f0 = g * P + j * HD
                            last = nc.tensor.matmul(state_ps[j * HD:(j + 1) * HD, g * HD:(g + 1) * HD],
                                                    Ktok[:, f0:f0 + HD], V[:, k % 2, f0:f0 + HD],
                                                    start=True, stop=True)
                    last.then_inc(state_done, 1)
                if ffn:
                    wait(pe, x1h_ready, c.count(k))
                    wait(pe, x1l_ready, c.count(k))
                    wait(pe, o_ready, c.count(k + 1))
                    three_pass(ffn_ps[:, :], lambda f: x1H[:, f, :], lambda f: x1L[:, f, :],
                               lambda f: WfH[:, f, :], lambda f: WfL[:, f, :]).then_inc(ffn_done, 1)
                if c.exists(k + 1):
                    n = k + 1
                    ncols = slice(n % QUAD * P, (n % QUAD + 1) * P)
                    vs = (n // QUAD) % 2
                    if not c.exists(k):
                        pe.wait_ge(wvh_ready, 1)
                        pe.wait_ge(wvl_ready, 1)
                    wait(pe, x1l_ready, c.count(k))
                    three_pass(v_ps[:, :], lambda f: xTH[:, vs, f, ncols], lambda f: xTL[:, vs, f, ncols],
                               lambda f: WvH[:, f, :], lambda f: WvL[:, f, :]).then_inc(v_done, 1)
                if c.exists(k + 8):
                    n = k + 8
                    wait(pe, xin_loaded[n % B], c.dma_count(n))
                    wait(pe, xl_ready, c.count(k + 8))
                    if proj:
                        wait(pe, k_ready, c.count(k + 5))
                    for g in range(NK):
                        last = nc.tensor.transpose(xtr_ps[:, g * P:(g + 1) * P],
                                                   xin[:, n % XIN, g * P:(g + 1) * P], ident[:])
                    last.then_inc(xtr_done, 1)

            run_slots(pe, slot, 8, 1, {-3: multiply_aux, -2: multiply_weight, -1: multiply_bv})

        @block.scalar
        def _(act):
            def split_wq_wk():
                act.wait_ge(wq_loaded, 16)
                nc.scalar.activation(WqH[:, :, :], wq_raw, ACT.Copy).then_inc(wqh_ready, 1)
                act.wait_ge(wk_loaded, 16)
                nc.scalar.activation(WkH[:, :, :], wk_raw, ACT.Copy).then_inc(wkh_ready, 1)
                act.wait_ge(biases_loaded, 48)
                act.wait_ge(bq_ready, 1)

            def split_wv_and_move_aux():
                act.wait_ge(wv_loaded, 16)
                nc.scalar.activation(WvH[:, :, :], wv_raw, ACT.Copy).then_inc(wvh_ready, 1)
                act.wait_ge(wql_ready, 1)
                for m in range(NK):
                    act.wait_ge(a12_done, m + 1)
                    nc.scalar.activation(a12[:, m, :], SC[:, m, :], ACT.Copy).then_inc(a12_ready, 1)

            def split_wf():
                for m in range(NK):
                    act.wait_ge(wf_done, m + 1)
                    nc.scalar.activation(WfH[:, m, :], SC[:, m, :], ACT.Copy).then_inc(wfh_ready, 1)
                act.wait_ge(wo_loaded, 16)
                nc.scalar.activation(WoH[:, :, :], wo_raw, ACT.Copy).then_inc(woh_ready, 1)

            def free_staging():
                act.wait_ge(c_ready, 1)
                act.wait_ge(wol_ready, 1)
                act.wait_ge(wvl_ready, 1)

            def slot(c, k):
                b = k % QUAD
                ns = 1 - (k // QUAD) % 2
                att = c.exists(k)
                ffn = c.exists(k - 1)
                proj = c.exists(k + 4)
                if att:
                    wait(act, scores_done, c.count(k + 1))
                    wait(act, num_done, c.count(k))
                    for j in range(HG):
                        nc.scalar.activation(A[:, j, :, :].rearrange("p g q -> p (g q)"), SC[:, j, :],
                                             ACT.Copy).then_inc(scores_out[j], 1)
                    wait(act, ktr_done, c.count(k + 1))
                    wait(act, state_done, c.count(k))
                    nc.scalar.activation(Ktok[:, :], ktr_ps[:, :], ACT.Copy).then_inc(ktok_ready, 1)
                if proj:
                    wait(act, qproj_done, c.count(k + 5))
                    wait(act, num_done, c.quad_count(k - 4))
                    nc.scalar.activation(QT[:, ns, b, :], qproj_ps[:, :], ACT.Exp,
                                         bias=bcol[:, 0, b:b + 1]).then_inc(q_ready, 1)
                if ffn:
                    wait(act, x1tr_done, c.count(k))
                    wait(act, ffn_done, c.count(k - 1))
                    nc.scalar.activation(x1H[:, :, :].rearrange("p g q -> p (g q)"), x1tr_ps[:, :],
                                         ACT.Copy).then_inc(x1h_ready, 1)
                if att:
                    wait(act, o_ready, c.count(k + 1))
                    wait(act, oproj_done, c.count(k))
                    nc.scalar.activation(oH[:, :, :], o[:, :, :], ACT.Copy).then_inc(oh_ready, 1)
                if c.exists(k + 1):
                    if c.exists(k):
                        wait(act, num_done, c.count(k + 1))
                    else:
                        act.wait_ge(consts_ready, 2)
                    wait(act, state_ready, c.count(k - 6))
                    for j in range(HG):
                        h = slice(j * HD, (j + 1) * HD)
                        last = nc.scalar.activation(stateB[h, :, h], state[h, (k + 1) % B, :, :], ACT.Copy)
                    last.then_inc(stateb_ready, 1)
                if proj:
                    wait(act, kproj_done, c.count(k + 5))
                    wait(act, num_done, c.quad_count(k - 4))
                    nc.scalar.activation(KT[:, ns, b, :], kproj_ps[:, :], ACT.Exp,
                                         bias=bcol[:, 1, b:b + 1]).then_inc(k_ready, 1)
                if c.exists(k + 1):
                    wait(act, qk1_ready, c.count(k + 2))
                    wait(act, den_done, c.count(k + 1))
                    nc.scalar.activation(qk1H[:, :], WK[:, 7, :], ACT.Copy).then_inc(qk1h_ready, 1)
                if ffn:
                    wait(act, z_ready, c.count(k))
                    nc.scalar.activation(z[:, :], z[:, :], ACT.Tanh).then_inc(tanh_ready, 1)
                if c.exists(k + 1):
                    wait(act, v_done, c.count(k + 2))
                    wait(act, state_done, c.count(k))
                    nc.scalar.activation(V[:, (k + 1) % 2, :], v_ps[:, :], ACT.Copy).then_inc(v_ready, 1)
                if c.exists(k + 8):
                    wait(act, xtr_done, c.count(k + 9))
                    nc.scalar.activation(xTH[:, (k // QUAD) % 2, :, b * P:(b + 1) * P],
                                         xtr_ps[:, :].rearrange("p (g q) -> p g q", g=NK),
                                         ACT.Copy).then_inc(xh_ready, 1)

            run_slots(act, slot, 8, 1, {-7: split_wq_wk, -3: split_wv_and_move_aux, -2: split_wf,
                                         -1: free_staging})

        @block.vector
        def _(dve):
            for n in range(HG):
                nc.vector.memset(blockones[n * HD:(n + 1) * HD, :], 0.0).then_inc(ones_zeroed, 1)
            dve.wait_ge(ones_zeroed, HG)
            for n in range(HG):
                last = nc.vector.memset(blockones[n * HD:(n + 1) * HD, n * HD:(n + 1) * HD], 1.0)
            last.then_inc(consts_ready, 1)
            dve.wait_ge(consts_ready, 1)
            nc.vector.tensor_copy(blockonesR[:], blockones[:])
            nc.vector.memset(state[:, :, :, :], 0.0)
            nc.vector.memset(stateB[:, :, :], 0.0)
            nc.vector.memset(k1[:, :, :], 0.0)
            nc.vector.memset(ones[:], 1.0)
            nc.vector.memset(bvrep, 1.0).then_inc(consts_ready, 1)
            dve.wait_ge(consts_ready, 2)

            def split_wq_wk():
                dve.wait_ge(biases_loaded, 48)
                nc.vector.tensor_scalar(bcol[:, 0, :], bcol[:, 0, :], -Q_SHIFT, None, ALU.add).then_inc(bq_ready, 1)
                for n in range(NK):
                    nc.vector.tensor_scalar(bvrep[:, n, :], bvrep[:, n, :], bcol[:, 2, n:n + 1], None,
                                            ALU.mult).then_inc(bvrep_ready, 1)
                dve.wait_ge(wqh_ready, 1)
                nc.vector.tensor_tensor(WqL[:, :, :], wq_raw, WqH[:, :, :].bitcast(F32),
                                        ALU.subtract).then_inc(wql_ready, 1)
                dve.wait_ge(wkh_ready, 1)
                nc.vector.tensor_tensor(WkL[:, :, :], wk_raw, WkH[:, :, :].bitcast(F32),
                                        ALU.subtract).then_inc(wkl_ready, 1)

            def split_wv():
                dve.wait_ge(wvh_ready, 1)
                nc.vector.tensor_tensor(WvL[:, :, :], wv_raw, WvH[:, :, :].bitcast(F32),
                                        ALU.subtract).then_inc(wvl_ready, 1)

            def split_wf_wo():
                for m in range(NK):
                    dve.wait_ge(wfh_ready, m + 1)
                    nc.vector.tensor_tensor(WfL[:, m, :], SC[:, m, :], WfH[:, m, :].bitcast(F32),
                                            ALU.subtract).then_inc(wfl_ready, 1)
                dve.wait_ge(woh_ready, 1)
                nc.vector.tensor_tensor(WoL[:, :, :], wo_raw, WoH[:, :, :].bitcast(F32),
                                        ALU.subtract).then_inc(wol_ready, 1)

            def add_bo():
                dve.wait_ge(small_loaded, 32)
                dve.wait_ge(c_done, 1)
                nc.vector.tensor_tensor(cbc[:, :], cbc[:, :], SC[:, 0, :], ALU.add).then_inc(c_ready, 1)

            def slot(c, k):
                b = k % QUAD
                bt = k % B
                if c.exists(k):
                    wait(dve, den_done, c.count(k + 1))
                    wait(dve, oh_ready, c.count(k))
                    wait(dve, ol_ready, c.count(k))
                    nc.vector.reciprocal(o[:, :, :].rearrange("p g q -> p (g q)"),
                                         den_ps[:, :]).then_inc(recip_ready, 1)
                if c.exists(k - 2):
                    wait(dve, y_ready, c.count(k - 1))
                    nc.vector.bn_stats(bnst[:, 1, :], y[:, k % 2, :]).then_inc(bn2_ready, 1)
                    wait_before(dve, (bn2_ready, c.count(k - 1)), (rstd2_ready, c.count(k - 2)))
                    nc.vector.bn_aggr(mv2[:, :], bnst[:, 1, :]).then_inc(stats2_ready, 1)
                if c.exists(k - 1):
                    wait(dve, oproj_done, c.count(k))
                    wait(dve, xb_ready, c.count(k))
                    wait(dve, x1_ready, c.count(k - 1))
                    nc.vector.tensor_tensor(r[:, :], oproj_ps[:, :], xres[:, (k - 1) % 2, :],
                                            ALU.add).then_inc(r_ready, 1)
                    wait(dve, r_ready, c.count(k))
                    nc.vector.bn_stats(bnst[:, 0, :], r[:, :]).then_inc(bn1_ready, 1)
                    wait_before(dve, (bn1_ready, c.count(k)))
                    nc.vector.bn_aggr(mv1[:, :], bnst[:, 0, :]).then_inc(stats1_ready, 1)
                if c.exists(k - 2):
                    wait(dve, rstd2_ready, c.count(k - 1))
                    wait(dve, stats2_ready, c.count(k - 1))
                    nc.vector.tensor_scalar(y[:, k % 2, :], y[:, k % 2, :], mv2[:, 0:1], rstd[:, 1:2],
                                            ALU.subtract, ALU.mult).then_inc(out_ready, 1)
                if c.exists(k - 1):
                    wait(dve, rstd1_ready, c.count(k))
                    wait(dve, y_ready, c.count(k - 2))
                    nc.vector.tensor_scalar(x1[:, (k - 1) % 2, :], r[:, :], mv1[:, 0:1], rstd[:, 0:1],
                                            ALU.subtract, ALU.mult).then_inc(x1_ready, 1)
                if c.exists(k):
                    wait(dve, num_done, c.count(k + 1))
                    wait(dve, recip_ready, c.count(k + 1))
                    oflat = o[:, :, :].rearrange("p g q -> p (g q)")
                    nc.vector.tensor_tensor(oflat, num_ps[:, :], oflat, ALU.mult).then_inc(o_ready, 1)
                if c.exists(k - 1):
                    wait(dve, x1h_ready, c.count(k))
                    nc.vector.tensor_tensor(x1L[:, :, :].rearrange("p g q -> p (g q)"), x1tr_ps[:, :],
                                            x1H[:, :, :].rearrange("p g q -> p (g q)").bitcast(F32),
                                            ALU.subtract).then_inc(x1l_ready, 1)
                if c.exists(k):
                    wait(dve, state_done, c.count(k + 1))
                    sflat = state[:, bt, :, :].rearrange("p g d -> p (g d)")
                    nc.vector.tensor_tensor(sflat, state_ps[:, 0:NK * HD], sflat, ALU.add).then_inc(state_ready, 1)
                if c.exists(k + 1):
                    n = k + 1
                    nb, nq = n % B, (n // QUAD) % 2
                    ncols = slice(n % QUAD * P, (n % QUAD + 1) * P)
                    wait(dve, k_ready, c.quad_count(n))
                    wait(dve, qk1l_ready, c.count(k + 1))
                    wait(dve, k1_ready, c.count(k - 6))
                    for g in range(NK):
                        last = nc.vector.tensor_tensor_scan(qk1[:, g, :], ones[:, :].to_broadcast([P, P]), KT[:, nq, g, ncols],
                                                            k1[:, nb, g:g + 1], ALU.mult, ALU.add)
                    last.then_inc(scan_ready, 1)
                    wait(dve, scan_ready, c.count(k + 2))
                    nc.vector.tensor_copy(k1[:, nb, :], qk1[:, :, P - 1]).then_inc(k1_ready, 1)
                    wait(dve, k1_ready, c.count(k + 2))
                    nc.vector.tensor_tensor(qk1[:, :, :], qk1[:, :, :], QT[:, nq, :, ncols],
                                            ALU.mult).then_inc(qk1_ready, 1)
                if c.exists(k - 1):
                    wait(dve, ffn_done, c.count(k))
                    wait(dve, y_ready, c.count(k - 1))
                    nc.vector.tensor_tensor(z[:, :], ffn_ps[:, :], bfbc[:, :], ALU.add).then_inc(z_ready, 1)
                if c.exists(k + 8):
                    xs = (k // QUAD) % 2
                    wait(dve, xh_ready, c.count(k + 9))
                    nc.vector.tensor_tensor(xTL[:, xs, :, b * P:(b + 1) * P],
                                            xtr_ps[:, :].rearrange("p (g q) -> p g q", g=NK),
                                            xTH[:, xs, :, b * P:(b + 1) * P].bitcast(F32),
                                            ALU.subtract).then_inc(xl_ready, 1)

            run_slots(dve, slot, 8, 2, {-7: split_wq_wk, -3: split_wv, -2: split_wf_wo, -1: add_bo})

        @block.gpsimd
        def _(pool):
            nc.gpsimd.memset(mhalf[:], -0.5)
            nc.gpsimd.memset(ident[:], 0.0).then_inc(ident_zeroed, 1)
            pool.wait_ge(ident_zeroed, 1)
            nc.gpsimd.affine_select(out=ident[:], in_=ident[:], compare_op=ALU.not_equal, fill=1.0, base=0,
                                    pattern=[[-1, P]], channel_multiplier=1).then_inc(ident_ready, 1)
            pool.wait_ge(ident_ready, 1)

            def slot(c, k):
                if c.exists(k - 2):
                    wait_before(pool, (stats2_ready, c.count(k - 1)))
                    nc.gpsimd.tensor_scalar(ve[:, 1:2], mv2[:, 1:2], EPS, None, ALU.add).then_inc(ve2_ready, 1)
                    wait(pool, ve2_ready, c.count(k - 1))
                    wait(pool, out_ready, c.count(k - 2))
                    nc.gpsimd.tensor_tensor(rstd[:, 1:2], ve[:, 1:2], mhalf[:, :], ALU.pow).then_inc(rstd2_ready, 1)
                if c.exists(k - 1):
                    wait_before(pool, (stats1_ready, c.count(k)))
                    nc.gpsimd.tensor_scalar(ve[:, 0:1], mv1[:, 1:2], EPS, None, ALU.add).then_inc(ve1_ready, 1)
                    wait(pool, ve1_ready, c.count(k))
                    wait(pool, x1_ready, c.count(k - 1))
                    nc.gpsimd.tensor_tensor(rstd[:, 0:1], ve[:, 0:1], mhalf[:, :], ALU.pow).then_inc(rstd1_ready, 1)
                if c.exists(k):
                    for j in range(HG):
                        wait_before(pool, (scores_out[j], c.count(k + 1)))
                        last = nc.gpsimd.affine_select(out=A[:, j, :, :], in_=A[:, j, :, :], compare_op=ALU.is_ge,
                                                fill=0.0, base=0, pattern=[[0, NK], [1, P]],
                                                channel_multiplier=-1)
                    last.then_inc(masked, 1)
                    wait(pool, oh_ready, c.count(k + 1))
                    wait(pool, oproj_done, c.count(k))
                    nc.gpsimd.tensor_tensor(oL[:, :, :], o[:, :, :], oH[:, :, :].bitcast(F32),
                                            ALU.subtract).then_inc(ol_ready, 1)
                if c.exists(k + 1):
                    wait(pool, qk1h_ready, c.count(k + 2))
                    nc.gpsimd.tensor_tensor(qk1L[:, :], WK[:, 7, :], qk1H[:, :].bitcast(F32),
                                            ALU.subtract).then_inc(qk1l_ready, 1)
                if c.exists(k - 1):
                    wait(pool, tanh_ready, c.count(k))
                    n = k - 1
                    wait(pool, out_stored[(k - 3) % B], c.dma_count(k - 3))
                    nc.gpsimd.tensor_tensor(y[:, n % 2, :], z[:, :], x1[:, n % 2, :], ALU.add).then_inc(y_ready, 1)
                if c.exists(k):
                    if not c.exists(k - 1):
                        pool.wait_ge(c_ready, 1)
                    wait(pool, xres_loaded[k], c.dma_count(k))
                    nc.gpsimd.tensor_tensor(xres[:, k % 2, :], xres[:, k % 2, :], cbc[:, :],
                                            ALU.add).then_inc(xb_ready, 1)

            run_slots(pool, slot, 1, 2)


def kernel(**inputs):
    import numpy as np
    import concourse.bacc as bacc
    from concourse.bass_utils import run_bass_kernel_spmd

    def by_partition(v):
        return np.ascontiguousarray(np.asarray(v).reshape(-1, 128).T)

    def transposed(m):
        return np.ascontiguousarray(np.asarray(m).T)

    arrays = {
        "x": np.ascontiguousarray(inputs["L0_attn_x"]),
        "wqT": transposed(inputs["L0_attn_Wq"]),
        "wkT": transposed(inputs["L0_attn_Wk"]),
        "wvT": transposed(inputs["L0_attn_Wv"]),
        "woT": transposed(inputs["L0_attn_Wo"]),
        "bq": by_partition(inputs["L0_attn_bq"]),
        "bk": by_partition(inputs["L0_attn_bk"]),
        "bv": by_partition(inputs["L0_attn_bv"]),
        "bo": np.ascontiguousarray(inputs["L0_attn_bo"]),
        "wT": transposed(inputs["L0_ffn_weight"]),
        "a1T": transposed(inputs["L0_ffn_aux_weight1"]),
        "a2": np.ascontiguousarray(inputs["L0_ffn_aux_weight2"]),
        "bf": np.ascontiguousarray(inputs["L0_ffn_bias"]),
    }
    nc = bacc.Bacc("TRN2", target_bir_lowering=False, num_devices=1)
    aps = [nc.dram_tensor(n, a.shape, mybir.dt.from_np(a.dtype), kind="ExternalInput").ap()
           for n, a in arrays.items()]
    out = nc.dram_tensor("out", arrays["x"].shape, mybir.dt.float32, kind="ExternalOutput").ap()
    linear_attention_ffn_kernel(nc, *aps, out)
    result = run_bass_kernel_spmd(nc, [arrays], core_ids=[0])
    return result.results[0]["out"]
```

```python
import concourse.bass as bass
from concourse import mybir
from contextlib import ExitStack


def linear_attention_ffn_kernel(nc, x, wqT, wkT, wvT, woT, bq, bk, bv, bo, w, a1T, a2, bf, out):
    F32 = mybir.dt.float32
    F32R = mybir.dt.float32r
    ALU = mybir.AluOpType
    ACT = mybir.ActivationFunctionType

    P = 128
    B, S, D = x.shape
    NK = D // P
    HD = 32
    HG = P // HD
    QUAD = 4
    NI = S // P
    NT = NI * B
    EPS = 1e-5
    Q_SHIFT = 8.0
    XIN = 2
    assert B == 2 * QUAD and NI >= 3

    x_t = x.rearrange("b (i p) d -> b i p d", p=P)
    out_t = out.rearrange("b (i p) d -> b i p d", p=P)

    ctx = ExitStack()
    with ctx:
        def sb(name, shape, dt=F32):
            return ctx.enter_context(nc.sbuf_tensor(name, shape, dt))

        def sem(name):
            return ctx.enter_context(nc.semaphore(name))

        WqH, WqL, WkH, WkL, WvH, WvL, WoH, WoL, WfH, WfL = [
            sb(n, [P, NK, D], F32R) for n in
            ("WqH", "WqL", "WkH", "WkL", "WvH", "WvL", "WoH", "WoL", "WfH", "WfL")]
        xin = sb("xin", [P, XIN, D])
        xres = sb("xres", [P, 2, D])
        xTH = sb("xTH", [P, 2, NK, QUAD * P], F32R)
        xTL = sb("xTL", [P, 2, NK, QUAD * P], F32R)
        QT = sb("QT", [P, 2, NK, QUAD * P])
        KT = sb("KT", [P, 2, NK, QUAD * P])
        V = sb("V", [P, 2, D])
        A = sb("A", [P, HG, NK, P])
        WK = sb("WK", [P, 8, D])
        r = WK[:, 0, :]
        z = WK[:, 1, :]
        y = WK[:, 2:4, :]
        x1 = WK[:, 4:6, :]
        Ktok = WK[:, 6, :]
        qk1 = WK[:, 7, :].rearrange("p (g q) -> p g q", g=NK)
        qk1H = sb("qk1H", [P, D], F32R)
        qk1L = sb("qk1L", [P, D], F32R)
        o = sb("o", [P, NK, P])
        oH = sb("oH", [P, NK, P], F32R)
        oL = sb("oL", [P, NK, P], F32R)
        x1H = sb("x1H", [P, NK, P], F32R)
        x1L = sb("x1L", [P, NK, P], F32R)
        state = sb("state", [P, B, NK, HD])
        stateB = sb("stateB", [P, NK, P])
        k1 = sb("k1", [P, B, NK])
        cbc = sb("cbc", [P, D])
        bfbc = sb("bfbc", [P, D])
        bcol = sb("bcol", [P, 3, NK])
        ident = sb("ident", [P, P])
        blockones = sb("blockones", [P, P])
        blockonesR = sb("blockonesR", [P, P], F32R)
        ones = sb("ones", [P, 1])
        bnst = sb("bnst", [P, 2, 6])
        mv1 = sb("mv1", [P, 2])
        mv2 = sb("mv2", [P, 2])
        ve = sb("ve", [P, 2])
        rstd = sb("rstd", [P, 2])
        mhalf = sb("mhalf", [P, 1])

        SC = ctx.enter_context(nc.psum_tensor("SC", [P, HG, NK * P], F32))
        G = [ctx.enter_context(nc.psum_tensor(f"G{i}", [P, D], F32)) for i in range(4)]
        den_ps, oproj_ps, ktr_ps, qproj_ps = G[0], G[1], G[2], G[3]
        num_ps, x1tr_ps, kproj_ps, state_ps = G[0], G[1], G[2], G[3]
        ffn_ps = G[0]

        den_done, scores_done, oproj_done, ktr_done, qproj_done, num_done, x1tr_done, kproj_done, state_done, \
            ffn_done, v_done, xtr_done = [sem(n) for n in (
                "den_done", "scores_done", "oproj_done", "ktr_done", "qproj_done", "num_done", "x1tr_done",
                "kproj_done", "state_done", "ffn_done", "v_done", "xtr_done")]
        scores_out = [sem(f"scores_out{j}") for j in range(HG)]
        ktok_ready, q_ready, k_ready, oh_ready, x1h_ready, tanh_ready, v_ready, xh_ready, qk1h_ready, \
            stateb_ready = [sem(n) for n in (
                "ktok_ready", "q_ready", "k_ready", "oh_ready", "x1h_ready", "tanh_ready", "v_ready", "xh_ready",
                "qk1h_ready", "stateb_ready")]
        recip_ready, r_ready, bn1_ready, stats1_ready, x1_ready, o_ready, x1l_ready, state_ready, qk1_ready, \
            z_ready, bn2_ready, stats2_ready, out_ready, xl_ready = [sem(n) for n in (
                "recip_ready", "r_ready", "bn1_ready", "stats1_ready", "x1_ready", "o_ready", "x1l_ready",
                "state_ready", "qk1_ready", "z_ready", "bn2_ready", "stats2_ready", "out_ready", "xl_ready")]
        scan_ready = sem("scan_ready")
        k1_ready = sem("k1_ready")
        masked = sem("masked")
        ve1_ready, rstd1_ready, ve2_ready, rstd2_ready, ol_ready, y_ready, xb_ready, \
            qk1l_ready = [sem(n) for n in (
            "ve1_ready", "rstd1_ready", "ve2_ready", "rstd2_ready", "ol_ready", "y_ready", "xb_ready",
                "qk1l_ready")]
        xin_loaded = [sem(f"xin_loaded{i}") for i in range(B)]
        xres_loaded = [sem(f"xres_loaded{i}") for i in range(B)]
        out_stored = [sem(f"out_stored{i}") for i in range(B)]
        small_loaded = sem("small_loaded")
        aux_loaded, w_loaded, wq_loaded, wk_loaded, wv_loaded, wo_loaded = [sem(n) for n in (
            "aux_loaded", "w_loaded", "wq_loaded", "wk_loaded", "wv_loaded", "wo_loaded")]
        a12_done, wf_done, c_done = sem("a12_done"), sem("wf_done"), sem("c_done")
        auxh_ready, auxl_ready, a12h_ready, a12l_ready, wh_ready, wl_ready = [sem(n) for n in (
            "auxh_ready", "auxl_ready", "a12h_ready", "a12l_ready", "wh_ready", "wl_ready")]
        wfh_ready, wfl_ready, c_ready = sem("wfh_ready"), sem("wfl_ready"), sem("c_ready")
        wqh_ready, wkh_ready, wvh_ready, woh_ready, wql_ready, wkl_ready, wvl_ready, wol_ready = [sem(n) for n in (
            "wqh_ready", "wkh_ready", "wvh_ready", "woh_ready", "wql_ready", "wkl_ready", "wvl_ready", "wol_ready")]
        biases_loaded = sem("biases_loaded")
        ones_zeroed, ident_zeroed, ident_ready, consts_ready, bvrep_ready, bq_ready = [sem(n) for n in (
            "ones_zeroed", "ident_zeroed", "ident_ready", "consts_ready", "bvrep_ready", "bq_ready")]

        wq_raw, wk_raw, a2_raw, w_raw = QT[:, 1], KT[:, 1], WK[:, 0:4, :], WK[:, 4:8, :]
        a1T_raw = A[:, :, :, :].rearrange("p h g q -> p h (g q)")
        wv_raw, wo_raw = wk_raw, a2_raw
        a1TH, a1TL, wH, wL = WvH, WvL, WfH, WfL
        a2H, a2L = WoH, WoL
        a12H, a12L = WoH, WoL
        bvrep = xres[:, 0, :].rearrange("p (k q) -> p k q", k=NK)

        def wait(engine, semaphore, value):
            if not isinstance(value, int) or value > 0:
                engine.wait_ge(semaphore, value)

        def wait_before(engine, *waits):
            engine.wait_ge(ident_ready, 1)
            for semaphore, value in waits:
                wait(engine, semaphore, value)

        class Chunk:

            def __init__(self, it, engine=None):
                self.it = it
                if engine is not None:
                    self.tiles = {n: engine.compute_val(it * B + n) for n in range(1 - B, 2 * B + 2)}
                    self.loads = {n: engine.compute_val(it * 16 + n * 16) for n in range(0, 3)}

            def count(self, n):
                return min(self.it * B + n, NT) if isinstance(self.it, int) else self.tiles[n]

            def state_count(self, n):
                return min(self.it * B + n, NT - B) if isinstance(self.it, int) else self.tiles[n]

            def reads_state(self):
                return not isinstance(self.it, int) or self.it > 0

            def updates_state(self):
                return not isinstance(self.it, int) or self.it < NI - 1

            def quad_count(self, n):
                return self.count((n // QUAD + 1) * QUAD)

            def dma_count(self, n):
                return (self.it + n // B + 1) * 16 if isinstance(self.it, int) else self.loads[n // B + 1]

            def exists(self, n):
                return not isinstance(self.it, int) or 0 <= B * self.it + n < NT

        def xtr_bank(c, k):
            return G[(k + 1) % 2] if isinstance(c.it, int) and c.it < 0 else G[2]

        def early_v(c, k):
            return c.exists(k) and c.exists(k + 1) and not c.exists(k + 4)

        def v_bank(c, k):
            return G[3] if early_v(c, k) else G[1]

        def run_slots(engine, slot, ahead, behind, setup={}):
            for t in range(-ahead, B):
                slot(Chunk(t // B), t % B)
                if t in setup:
                    setup[t]()
            with engine.Fori(1, NI - 1) as it:
                c = Chunk(it, engine)
                for k in range(B):
                    slot(c, k)
            for t in range(NT - B, NT + behind):
                slot(Chunk(t // B), t % B)

        block = ctx.enter_context(nc.Block())

        @block.sync
        def _(sp):
            def wview(a):
                return a.rearrange("(k p) n -> p k n", p=P)

            def load_wq_and_biases():
                sp.dma_start(bcol[:, 0, :], bq).then_inc(biases_loaded, 16)
                sp.dma_start(bcol[:, 1, :], bk).then_inc(biases_loaded, 16)
                sp.dma_start(bcol[:, 2, :], bv).then_inc(biases_loaded, 16)
                sp.dma_start(wq_raw, wview(wqT)).then_inc(wq_loaded, 16)

            def load_wk():
                sp.dma_start(wk_raw, wview(wkT)).then_inc(wk_loaded, 16)

            def load_ffn_weights_and_wv():
                sp.dma_start(a1T_raw, wview(a1T)).then_inc(aux_loaded, 16)
                sp.dma_start(a2_raw, wview(a2)).then_inc(aux_loaded, 16)
                sp.dma_start(w_raw, wview(w)).then_inc(w_loaded, 16)
                sp.dma_start(cbc[:], bo.partition_broadcast(P)).then_inc(small_loaded, 16)
                sp.dma_start(bfbc[:], bf.partition_broadcast(P)).then_inc(small_loaded, 16)
                sp.wait_ge(wkl_ready, 1)
                sp.dma_start(wv_raw, wview(wvT)).then_inc(wv_loaded, 16)

            def load_wo():
                sp.wait_ge(auxl_ready, 2)
                sp.dma_start(wo_raw, wview(woT)).then_inc(wo_loaded, 16)

            def slot(c, k):
                if c.exists(k + 8):
                    wait_before(sp, (xtr_done, c.count(k + 7)))
                    n = k + 8
                    sp.dma_start(xin[:, n % XIN, :], x_t[n % B, c.it + n // B]).then_inc(xin_loaded[n % B], 16)
                if c.exists(k + 1):
                    if isinstance(c.it, int) and c.it * B + k == -1:
                        sp.wait_ge(c_done, 1)
                    wait_before(sp, (r_ready, c.count(k)))
                    n = k + 1
                    sp.dma_start(xres[:, n % 2, :], x_t[n % B, c.it + n // B]).then_inc(xres_loaded[n % B], 16)
                if c.exists(k - 2):
                    wait_before(sp, (out_ready, c.count(k - 1)))
                    n = k - 2
                    sp.dma_start(out_t[n % B, c.it + n // B], y[:, n % 2, :]).then_inc(out_stored[n % B], 16)

            run_slots(sp, slot, 8, 2, {-7: load_wq_and_biases, -5: load_wk, -4: load_ffn_weights_and_wv,
                                        -2: load_wo})
            for n in range(B):
                sp.wait_ge(out_stored[n], 16 * NI)

        @block.tensor
        def _(pe):
            def three_pass(out, statH, statL, movH, movL):
                for k in range(NK):
                    nc.tensor.matmul(out, statH(k), movH(k), start=(k == 0), stop=False)
                    nc.tensor.matmul(out, statH(k), movL(k), start=False, stop=False)
                    last = nc.tensor.matmul(out, statL(k), movH(k), start=False, stop=(k == NK - 1))
                return last

            def multiply_aux():
                pe.wait_ge(auxh_ready, 2)
                pe.wait_ge(auxl_ready, 2)
                for m in range(NK):
                    cols = slice(m * P, (m + 1) * P)
                    three_pass(SC[:, m, :], lambda f: a1TH[:, f, cols], lambda f: a1TL[:, f, cols],
                               lambda f: a2H[:, f, :], lambda f: a2L[:, f, :]).then_inc(a12_done, 1)

            def multiply_weight():
                pe.wait_ge(a12h_ready, NK)
                pe.wait_ge(a12l_ready, NK)
                pe.wait_ge(wh_ready, 1)
                pe.wait_ge(wl_ready, 1)
                for m in range(NK):
                    cols = slice(m * P, (m + 1) * P)
                    three_pass(SC[:, m, :], lambda f: wH[:, f, cols], lambda f: wL[:, f, cols],
                               lambda f: a12H[:, f, :], lambda f: a12L[:, f, :]).then_inc(wf_done, 1)

            def multiply_bv():
                pe.wait_ge(bvrep_ready, NK)
                pe.wait_ge(wo_loaded, 16)
                pe.wait_ge(wfl_ready, NK)
                for k in range(NK):
                    last = nc.tensor.matmul(SC[:, 0, :], bvrep[:, k, :], wo_raw[:, k, :],
                                            start=(k == 0), stop=(k == NK - 1))
                last.then_inc(c_done, 1)
                pe.wait_ge(c_ready, 1)
                pe.wait_ge(consts_ready, 2)

            pe.wait_ge(ident_ready, 1)

            def slot(c, k):
                b = k % QUAD
                s = (k // QUAD) % 2
                cols = slice(b * P, (b + 1) * P)
                att = c.exists(k)
                ffn = c.exists(k - 1)
                proj = c.exists(k + 4)

                def scores(groups):
                    for g in groups:
                        for j in range(HG):
                            h = slice(j * HD, (j + 1) * HD)
                            last = nc.tensor.matmul(SC[:, j, g * P:(g + 1) * P], KT[h, s, g, cols],
                                                    QT[h, s, g, cols], start=True, stop=True)
                    return last

                def v_projection():
                    ncols = slice((k + 1) % QUAD * P, ((k + 1) % QUAD + 1) * P)
                    vs = ((k + 1) // QUAD) % 2
                    three_pass(v_bank(c, k)[:, :], lambda f: xTH[:, vs, f, ncols], lambda f: xTL[:, vs, f, ncols],
                               lambda f: WvH[:, f, :], lambda f: WvL[:, f, :]).then_inc(v_done, 1)

                def denominator():
                    wait(pe, qk1h_ready, c.count(k + 1))
                    wait(pe, qk1l_ready, c.count(k + 1))
                    wait(pe, z_ready, c.count(k - 1))
                    if not c.exists(k - 1):
                        wait(pe, xl_ready, c.count(k + 8))
                    nc.tensor.matmul(den_ps[:, :], blockonesR[:], qk1H[:, :], start=True, stop=False)
                    nc.tensor.matmul(den_ps[:, :], blockonesR[:], qk1L[:, :], start=False,
                                     stop=True).then_inc(den_done, 1)

                late_den = early_v(c, k - 1)
                if att and not late_den:
                    denominator()
                if att:
                    wait(pe, k_ready, c.quad_count(k))
                    for j in range(HG):
                        wait(pe, scores_out[j], c.count(k))
                    scores(range(0, NK // 2))
                if att and late_den:
                    denominator()
                if ffn:
                    if not c.exists(k - 2):
                        pe.wait_ge(woh_ready, 1)
                        pe.wait_ge(wol_ready, 1)
                    wait(pe, oh_ready, c.count(k))
                    wait(pe, ol_ready, c.count(k))
                    wait(pe, v_ready, c.count(k + 1))
                    three_pass(oproj_ps[:, :], lambda f: oH[:, f, :], lambda f: oL[:, f, :],
                               lambda f: WoH[:, f, :], lambda f: WoL[:, f, :]).then_inc(oproj_done, 1)
                if att:
                    scores(range(NK // 2, NK)).then_inc(scores_done, 1)
                if att and c.updates_state():
                    wait(pe, xl_ready, c.count(k + 8))
                    for g in range(NK):
                        last = nc.tensor.transpose(ktr_ps[:, g * P:(g + 1) * P], KT[:, s, g, cols], ident[:])
                    last.then_inc(ktr_done, 1)
                if early_v(c, k):
                    wait(pe, q_ready, c.count(k + 4))
                    wait(pe, v_ready, c.count(k + 1))
                    v_projection()
                if proj:
                    ns = 1 - s
                    if not c.exists(k + 3):
                        pe.wait_ge(wqh_ready, 1)
                        pe.wait_ge(wql_ready, 1)
                    wait(pe, xl_ready, c.quad_count(k + 4))
                    if att:
                        wait(pe, state_ready, c.state_count(k))
                    if not att or not c.updates_state():
                        wait(pe, q_ready, c.count(k + 4))
                    three_pass(qproj_ps[:, :], lambda f: WqH[:, f, b * P:(b + 1) * P],
                               lambda f: WqL[:, f, b * P:(b + 1) * P], lambda f: xTH[:, ns, f, :],
                               lambda f: xTL[:, ns, f, :]).then_inc(qproj_done, 1)
                if att and c.reads_state():
                    wait(pe, recip_ready, c.count(k + 1))
                    wait(pe, stateb_ready, c.count(k + 1))
                    for g in range(NK):
                        nc.tensor.matmul(num_ps[:, g * P:(g + 1) * P], stateB[:, g, :], QT[:, s, g, cols],
                                         start=(g == 0), stop=False, skip_group_check=True)
                if ffn:
                    wait(pe, x1_ready, c.count(k))
                    wait(pe, r_ready, c.count(k))
                    for g in range(NK):
                        last = nc.tensor.transpose(x1tr_ps[:, g * P:(g + 1) * P],
                                                   x1[:, (k - 1) % 2, g * P:(g + 1) * P], ident[:])
                    last.then_inc(x1tr_done, 1)
                if att:
                    wait(pe, v_ready, c.count(k + 1))
                    if not c.reads_state():
                        wait(pe, recip_ready, c.count(k + 1))
                    wait(pe, masked, c.count(k + 1))
                    for g in range(NK):
                        for j in range(HG):
                            h = slice(j * HD, (j + 1) * HD)
                            f0 = g * P + j * HD
                            last = nc.tensor.matmul(num_ps[h, g * P:(g + 1) * P], V[:, k % 2, f0:f0 + HD],
                                                    A[:, j, g, :], start=(g == 0 and not c.reads_state()), stop=True,
                                                    skip_group_check=True)
                    last.then_inc(num_done, 1)
                if att and c.updates_state():
                    wait(pe, ktok_ready, c.count(k + 1))
                    wait(pe, q_ready, c.count(k + 5))
                    for g in range(NK):
                        for j in range(HG):
                            f0 = g * P + j * HD
                            last = nc.tensor.matmul(state_ps[j * HD:(j + 1) * HD, g * HD:(g + 1) * HD],
                                                    Ktok[:, f0:f0 + HD], V[:, k % 2, f0:f0 + HD],
                                                    start=True, stop=True)
                    last.then_inc(state_done, 1)
                if proj:
                    if not c.exists(k + 3):
                        pe.wait_ge(wkh_ready, 1)
                        pe.wait_ge(wkl_ready, 1)
                    if att and c.updates_state():
                        wait(pe, ktok_ready, c.count(k + 1))
                    else:
                        if att:
                            wait(pe, xl_ready, c.count(k + 8))
                        wait(pe, k_ready, c.count(k + 4))
                    three_pass(kproj_ps[:, :], lambda f: WkH[:, f, b * P:(b + 1) * P],
                               lambda f: WkL[:, f, b * P:(b + 1) * P], lambda f: xTH[:, ns, f, :],
                               lambda f: xTL[:, ns, f, :]).then_inc(kproj_done, 1)
                if ffn:
                    wait(pe, x1h_ready, c.count(k))
                    wait(pe, x1l_ready, c.count(k))
                    wait(pe, o_ready, c.count(k + 1))
                    three_pass(ffn_ps[:, :], lambda f: x1H[:, f, :], lambda f: x1L[:, f, :],
                               lambda f: WfH[:, f, :], lambda f: WfL[:, f, :]).then_inc(ffn_done, 1)
                if c.exists(k + 1) and not early_v(c, k):
                    if not c.exists(k):
                        pe.wait_ge(wvh_ready, 1)
                        pe.wait_ge(wvl_ready, 1)
                    wait(pe, x1l_ready, c.count(k))
                    if not att:
                        wait(pe, xl_ready, c.count(k + 8))
                    v_projection()
                if c.exists(k + 8):
                    n = k + 8
                    wait(pe, xin_loaded[n % B], c.dma_count(n))
                    if att:
                        wait(pe, xl_ready, c.count(k + 8))
                        wait(pe, k_ready, c.count(k + 5))
                    else:
                        wait(pe, xl_ready, c.count(k + 7))
                    for g in range(NK):
                        last = nc.tensor.transpose(xtr_bank(c, k)[:, g * P:(g + 1) * P],
                                                   xin[:, n % XIN, g * P:(g + 1) * P], ident[:])
                    last.then_inc(xtr_done, 1)

            run_slots(pe, slot, 8, 1, {-3: multiply_aux, -2: multiply_weight, -1: multiply_bv})

        @block.scalar
        def _(act):
            def split_wq():
                act.wait_ge(wq_loaded, 16)
                nc.scalar.activation(WqH[:, :, :], wq_raw, ACT.Copy).then_inc(wqh_ready, 1)
                act.wait_ge(biases_loaded, 48)
                act.wait_ge(bq_ready, 1)

            def split_wk():
                act.wait_ge(wk_loaded, 16)
                nc.scalar.activation(WkH[:, :, :], wk_raw, ACT.Copy).then_inc(wkh_ready, 1)

            def split_aux():
                act.wait_ge(aux_loaded, 32)
                nc.scalar.activation(a1TH[:, :, :], a1T_raw, ACT.Copy).then_inc(auxh_ready, 1)
                nc.scalar.activation(a2H[:, :, :], a2_raw, ACT.Copy).then_inc(auxh_ready, 1)

            def split_a12():
                act.wait_ge(w_loaded, 16)
                nc.scalar.activation(wH[:, :, :], w_raw, ACT.Copy).then_inc(wh_ready, 1)
                act.wait_ge(a12_done, NK)
                for m in range(NK):
                    nc.scalar.activation(a12H[:, m, :], SC[:, m, :], ACT.Copy).then_inc(a12h_ready, 1)

            def split_wv_wf_wo():
                act.wait_ge(wv_loaded, 16)
                nc.scalar.activation(WvH[:, :, :], wv_raw, ACT.Copy).then_inc(wvh_ready, 1)
                act.wait_ge(wf_done, NK)
                for m in range(NK):
                    nc.scalar.activation(WfH[:, m, :], SC[:, m, :], ACT.Copy).then_inc(wfh_ready, 1)
                act.wait_ge(wo_loaded, 16)
                nc.scalar.activation(WoH[:, :, :], wo_raw, ACT.Copy).then_inc(woh_ready, 1)

            def free_staging():
                act.wait_ge(c_ready, 1)
                act.wait_ge(wol_ready, 1)
                act.wait_ge(wvl_ready, 1)

            def slot(c, k):
                b = k % QUAD
                ns = 1 - (k // QUAD) % 2
                att = c.exists(k)
                ffn = c.exists(k - 1)
                proj = c.exists(k + 4)

                def copy_v():
                    wait(act, v_done, c.count(k + 2))
                    wait(act, state_done, c.state_count(k))
                    wait(act, num_done, c.count(k))
                    nc.scalar.activation(V[:, (k + 1) % 2, :], v_bank(c, k)[:, :], ACT.Copy).then_inc(v_ready, 1)

                if att:
                    wait(act, scores_done, c.count(k + 1))
                    wait(act, num_done, c.count(k))
                    for j in range(HG):
                        nc.scalar.activation(A[:, j, :, :].rearrange("p g q -> p (g q)"), SC[:, j, :],
                                             ACT.Copy).then_inc(scores_out[j], 1)
                if att and c.updates_state():
                    wait(act, ktr_done, c.count(k + 1))
                    wait(act, state_done, c.count(k))
                    nc.scalar.activation(Ktok[:, :], ktr_ps[:, :], ACT.Copy).then_inc(ktok_ready, 1)
                if proj:
                    wait(act, qproj_done, c.count(k + 5))
                    wait(act, num_done, c.quad_count(k - 4))
                    nc.scalar.activation(QT[:, ns, b, :], qproj_ps[:, :], ACT.Exp,
                                         bias=bcol[:, 0, b:b + 1]).then_inc(q_ready, 1)
                if early_v(c, k):
                    copy_v()
                if ffn:
                    wait(act, x1tr_done, c.count(k))
                    wait(act, ffn_done, c.count(k - 1))
                    nc.scalar.activation(x1H[:, :, :].rearrange("p g q -> p (g q)"), x1tr_ps[:, :],
                                         ACT.Copy).then_inc(x1h_ready, 1)
                if att:
                    wait(act, o_ready, c.count(k + 1))
                    wait(act, oproj_done, c.count(k))
                    nc.scalar.activation(oH[:, :, :], o[:, :, :], ACT.Copy).then_inc(oh_ready, 1)
                if c.exists(k + 1):
                    if c.exists(k):
                        wait(act, num_done, c.count(k + 1))
                    else:
                        act.wait_ge(consts_ready, 2)
                    wait(act, state_ready, c.count(k - 6))
                    for j in range(HG):
                        h = slice(j * HD, (j + 1) * HD)
                        last = nc.scalar.activation(stateB[h, :, h], state[h, (k + 1) % B, :, :], ACT.Copy)
                    last.then_inc(stateb_ready, 1)
                if proj:
                    wait(act, kproj_done, c.count(k + 5))
                    wait(act, num_done, c.quad_count(k - 4))
                    nc.scalar.activation(KT[:, ns, b, :], kproj_ps[:, :], ACT.Exp,
                                         bias=bcol[:, 1, b:b + 1]).then_inc(k_ready, 1)
                if c.exists(k + 1):
                    wait(act, qk1_ready, c.count(k + 2))
                    wait(act, den_done, c.count(k + 1))
                    nc.scalar.activation(qk1H[:, :], WK[:, 7, :], ACT.Copy).then_inc(qk1h_ready, 1)
                if ffn:
                    wait(act, z_ready, c.count(k))
                    nc.scalar.activation(z[:, :], z[:, :], ACT.Tanh).then_inc(tanh_ready, 1)
                if c.exists(k + 1) and not early_v(c, k):
                    copy_v()
                if c.exists(k + 8):
                    wait(act, xtr_done, c.count(k + 9))
                    nc.scalar.activation(xTH[:, (k // QUAD) % 2, :, b * P:(b + 1) * P],
                                         xtr_bank(c, k)[:, :].rearrange("p (g q) -> p g q", g=NK),
                                         ACT.Copy).then_inc(xh_ready, 1)

            run_slots(act, slot, 8, 1, {-7: split_wq, -5: split_wk, -4: split_aux, -3: split_a12,
                                        -2: split_wv_wf_wo, -1: free_staging})

        @block.vector
        def _(dve):
            for n in range(HG):
                nc.vector.memset(blockones[n * HD:(n + 1) * HD, :], 0.0).then_inc(ones_zeroed, 1)
            dve.wait_ge(ones_zeroed, HG)
            for n in range(HG):
                last = nc.vector.memset(blockones[n * HD:(n + 1) * HD, n * HD:(n + 1) * HD], 1.0)
            last.then_inc(consts_ready, 1)
            dve.wait_ge(consts_ready, 1)
            nc.vector.tensor_copy(blockonesR[:], blockones[:])
            nc.vector.memset(state[:, :, :, :], 0.0)
            nc.vector.memset(stateB[:, :, :], 0.0)
            nc.vector.memset(k1[:, :, :], 0.0)
            nc.vector.memset(ones[:], 1.0)
            nc.vector.memset(bvrep, 1.0).then_inc(consts_ready, 1)
            dve.wait_ge(consts_ready, 2)

            def split_wq():
                dve.wait_ge(biases_loaded, 48)
                nc.vector.tensor_scalar(bcol[:, 0, :], bcol[:, 0, :], -Q_SHIFT, None, ALU.add).then_inc(bq_ready, 1)
                for n in range(NK):
                    nc.vector.tensor_scalar(bvrep[:, n, :], bvrep[:, n, :], bcol[:, 2, n:n + 1], None,
                                            ALU.mult).then_inc(bvrep_ready, 1)
                dve.wait_ge(wqh_ready, 1)
                nc.vector.tensor_tensor(WqL[:, :, :], wq_raw, WqH[:, :, :].bitcast(F32),
                                        ALU.subtract).then_inc(wql_ready, 1)

            def split_wk():
                dve.wait_ge(wkh_ready, 1)
                nc.vector.tensor_tensor(WkL[:, :, :], wk_raw, WkH[:, :, :].bitcast(F32),
                                        ALU.subtract).then_inc(wkl_ready, 1)

            def split_aux():
                dve.wait_ge(auxh_ready, 1)
                nc.vector.tensor_tensor(a1TL[:, :, :], a1T_raw, a1TH[:, :, :].bitcast(F32),
                                        ALU.subtract).then_inc(auxl_ready, 1)
                dve.wait_ge(auxh_ready, 2)
                nc.vector.tensor_tensor(a2L[:, :, :], a2_raw, a2H[:, :, :].bitcast(F32),
                                        ALU.subtract).then_inc(auxl_ready, 1)

            def split_a12():
                dve.wait_ge(wh_ready, 1)
                nc.vector.tensor_tensor(wL[:, :, :], w_raw, wH[:, :, :].bitcast(F32),
                                        ALU.subtract).then_inc(wl_ready, 1)
                for m in range(NK):
                    dve.wait_ge(a12h_ready, m + 1)
                    nc.vector.tensor_tensor(a12L[:, m, :], SC[:, m, :], a12H[:, m, :].bitcast(F32),
                                            ALU.subtract).then_inc(a12l_ready, 1)

            def split_wv_wf_wo():
                dve.wait_ge(wvh_ready, 1)
                nc.vector.tensor_tensor(WvL[:, :, :], wv_raw, WvH[:, :, :].bitcast(F32),
                                        ALU.subtract).then_inc(wvl_ready, 1)
                for m in range(NK):
                    dve.wait_ge(wfh_ready, m + 1)
                    nc.vector.tensor_tensor(WfL[:, m, :], SC[:, m, :], WfH[:, m, :].bitcast(F32),
                                            ALU.subtract).then_inc(wfl_ready, 1)
                dve.wait_ge(woh_ready, 1)
                nc.vector.tensor_tensor(WoL[:, :, :], wo_raw, WoH[:, :, :].bitcast(F32),
                                        ALU.subtract).then_inc(wol_ready, 1)

            def add_bo():
                dve.wait_ge(small_loaded, 32)
                dve.wait_ge(c_done, 1)
                nc.vector.tensor_tensor(cbc[:, :], cbc[:, :], SC[:, 0, :], ALU.add).then_inc(c_ready, 1)

            def slot(c, k):
                b = k % QUAD
                bt = k % B
                if c.exists(k):
                    wait(dve, den_done, c.count(k + 1))
                    wait(dve, oh_ready, c.count(k))
                    wait(dve, ol_ready, c.count(k))
                    nc.vector.reciprocal(o[:, :, :].rearrange("p g q -> p (g q)"),
                                         den_ps[:, :]).then_inc(recip_ready, 1)
                if c.exists(k - 2):
                    wait(dve, y_ready, c.count(k - 1))
                    nc.vector.bn_stats(bnst[:, 1, :], y[:, k % 2, :]).then_inc(bn2_ready, 1)
                    wait_before(dve, (bn2_ready, c.count(k - 1)), (rstd2_ready, c.count(k - 2)))
                    nc.vector.bn_aggr(mv2[:, :], bnst[:, 1, :]).then_inc(stats2_ready, 1)
                if c.exists(k - 1):
                    wait(dve, oproj_done, c.count(k))
                    wait(dve, xb_ready, c.count(k))
                    wait(dve, x1_ready, c.count(k - 1))
                    nc.vector.tensor_tensor(r[:, :], oproj_ps[:, :], xres[:, (k - 1) % 2, :],
                                            ALU.add).then_inc(r_ready, 1)
                    wait(dve, r_ready, c.count(k))
                    nc.vector.bn_stats(bnst[:, 0, :], r[:, :]).then_inc(bn1_ready, 1)
                    wait_before(dve, (bn1_ready, c.count(k)))
                    nc.vector.bn_aggr(mv1[:, :], bnst[:, 0, :]).then_inc(stats1_ready, 1)
                if c.exists(k - 2):
                    wait(dve, rstd2_ready, c.count(k - 1))
                    wait(dve, stats2_ready, c.count(k - 1))
                    nc.vector.tensor_scalar(y[:, k % 2, :], y[:, k % 2, :], mv2[:, 0:1], rstd[:, 1:2],
                                            ALU.subtract, ALU.mult).then_inc(out_ready, 1)
                if c.exists(k - 1):
                    wait(dve, rstd1_ready, c.count(k))
                    wait(dve, y_ready, c.count(k - 2))
                    nc.vector.tensor_scalar(x1[:, (k - 1) % 2, :], r[:, :], mv1[:, 0:1], rstd[:, 0:1],
                                            ALU.subtract, ALU.mult).then_inc(x1_ready, 1)
                if c.exists(k - 1):
                    wait(dve, x1h_ready, c.count(k))
                    nc.vector.tensor_tensor(x1L[:, :, :].rearrange("p g q -> p (g q)"), x1tr_ps[:, :],
                                            x1H[:, :, :].rearrange("p g q -> p (g q)").bitcast(F32),
                                            ALU.subtract).then_inc(x1l_ready, 1)
                if c.exists(k):
                    wait(dve, num_done, c.count(k + 1))
                    wait(dve, recip_ready, c.count(k + 1))
                    oflat = o[:, :, :].rearrange("p g q -> p (g q)")
                    nc.vector.tensor_tensor(oflat, num_ps[:, :], oflat, ALU.mult).then_inc(o_ready, 1)
                if c.exists(k) and c.updates_state():
                    wait(dve, state_done, c.count(k + 1))
                    sflat = state[:, bt, :, :].rearrange("p g d -> p (g d)")
                    nc.vector.tensor_tensor(sflat, state_ps[:, 0:NK * HD], sflat, ALU.add).then_inc(state_ready, 1)
                if c.exists(k + 1):
                    n = k + 1
                    nb, nq = n % B, (n // QUAD) % 2
                    ncols = slice(n % QUAD * P, (n % QUAD + 1) * P)
                    wait(dve, k_ready, c.quad_count(n))
                    wait(dve, qk1l_ready, c.count(k + 1))
                    wait(dve, k1_ready, c.count(k - 6))
                    for g in range(NK):
                        last = nc.vector.tensor_tensor_scan(qk1[:, g, :], ones[:, :].to_broadcast([P, P]),
                                                            KT[:, nq, g, ncols], k1[:, nb, g:g + 1],
                                                            ALU.mult, ALU.add)
                    last.then_inc(scan_ready, 1)
                    wait(dve, scan_ready, c.count(k + 2))
                    nc.vector.tensor_copy(k1[:, nb, :], qk1[:, :, P - 1]).then_inc(k1_ready, 1)
                    wait(dve, k1_ready, c.count(k + 2))
                    nc.vector.tensor_tensor(qk1[:, :, :], qk1[:, :, :], QT[:, nq, :, ncols],
                                            ALU.mult).then_inc(qk1_ready, 1)
                if c.exists(k - 1):
                    wait(dve, ffn_done, c.count(k))
                    wait(dve, y_ready, c.count(k - 1))
                    nc.vector.tensor_tensor(z[:, :], ffn_ps[:, :], bfbc[:, :], ALU.add).then_inc(z_ready, 1)
                if c.exists(k + 8):
                    xs = (k // QUAD) % 2
                    wait(dve, xh_ready, c.count(k + 9))
                    nc.vector.tensor_tensor(xTL[:, xs, :, b * P:(b + 1) * P],
                                            xtr_bank(c, k)[:, :].rearrange("p (g q) -> p g q", g=NK),
                                            xTH[:, xs, :, b * P:(b + 1) * P].bitcast(F32),
                                            ALU.subtract).then_inc(xl_ready, 1)

            run_slots(dve, slot, 8, 2, {-7: split_wq, -5: split_wk, -4: split_aux,
                                       -3: split_a12, -2: split_wv_wf_wo, -1: add_bo})

        @block.gpsimd
        def _(pool):
            nc.gpsimd.memset(mhalf[:], -0.5)
            nc.gpsimd.memset(ident[:], 0.0).then_inc(ident_zeroed, 1)
            pool.wait_ge(ident_zeroed, 1)
            nc.gpsimd.affine_select(out=ident[:], in_=ident[:], compare_op=ALU.not_equal, fill=1.0, base=0,
                                    pattern=[[-1, P]], channel_multiplier=1).then_inc(ident_ready, 1)
            pool.wait_ge(ident_ready, 1)

            def slot(c, k):
                if c.exists(k - 2):
                    wait_before(pool, (stats2_ready, c.count(k - 1)))
                    nc.gpsimd.tensor_scalar(ve[:, 1:2], mv2[:, 1:2], EPS, None, ALU.add).then_inc(ve2_ready, 1)
                    wait(pool, ve2_ready, c.count(k - 1))
                    wait(pool, out_ready, c.count(k - 2))
                    nc.gpsimd.tensor_tensor(rstd[:, 1:2], ve[:, 1:2], mhalf[:, :], ALU.pow).then_inc(rstd2_ready, 1)
                if c.exists(k - 1):
                    wait_before(pool, (stats1_ready, c.count(k)))
                    nc.gpsimd.tensor_scalar(ve[:, 0:1], mv1[:, 1:2], EPS, None, ALU.add).then_inc(ve1_ready, 1)
                    wait(pool, ve1_ready, c.count(k))
                    wait(pool, x1_ready, c.count(k - 1))
                    nc.gpsimd.tensor_tensor(rstd[:, 0:1], ve[:, 0:1], mhalf[:, :], ALU.pow).then_inc(rstd1_ready, 1)
                if c.exists(k):
                    for j in range(HG):
                        wait_before(pool, (scores_out[j], c.count(k + 1)))
                        last = nc.gpsimd.affine_select(out=A[:, j, :, :], in_=A[:, j, :, :], compare_op=ALU.is_ge,
                                                fill=0.0, base=0, pattern=[[0, NK], [1, P]],
                                                channel_multiplier=-1)
                    last.then_inc(masked, 1)
                    wait(pool, oh_ready, c.count(k + 1))
                    wait(pool, oproj_done, c.count(k))
                    nc.gpsimd.tensor_tensor(oL[:, :, :], o[:, :, :], oH[:, :, :].bitcast(F32),
                                            ALU.subtract).then_inc(ol_ready, 1)
                if c.exists(k + 1):
                    wait(pool, qk1h_ready, c.count(k + 2))
                    nc.gpsimd.tensor_tensor(qk1L[:, :], WK[:, 7, :], qk1H[:, :].bitcast(F32),
                                            ALU.subtract).then_inc(qk1l_ready, 1)
                if c.exists(k - 1):
                    wait(pool, tanh_ready, c.count(k))
                    n = k - 1
                    wait(pool, out_stored[(k - 3) % B], c.dma_count(k - 3))
                    nc.gpsimd.tensor_tensor(y[:, n % 2, :], z[:, :], x1[:, n % 2, :], ALU.add).then_inc(y_ready, 1)
                if c.exists(k):
                    if not c.exists(k - 1):
                        pool.wait_ge(c_ready, 1)
                    wait(pool, xres_loaded[k], c.dma_count(k))
                    nc.gpsimd.tensor_tensor(xres[:, k % 2, :], xres[:, k % 2, :], cbc[:, :],
                                            ALU.add).then_inc(xb_ready, 1)

            run_slots(pool, slot, 1, 2)


def kernel(**inputs):
    import numpy as np
    import concourse.bacc as bacc
    from concourse.bass_utils import run_bass_kernel_spmd

    def by_partition(v):
        return np.ascontiguousarray(np.asarray(v).reshape(-1, 128).T)

    def transposed(m):
        return np.ascontiguousarray(np.asarray(m).T)

    arrays = {
        "x": np.ascontiguousarray(inputs["L0_attn_x"]),
        "wqT": transposed(inputs["L0_attn_Wq"]),
        "wkT": transposed(inputs["L0_attn_Wk"]),
        "wvT": transposed(inputs["L0_attn_Wv"]),
        "woT": transposed(inputs["L0_attn_Wo"]),
        "bq": by_partition(inputs["L0_attn_bq"]),
        "bk": by_partition(inputs["L0_attn_bk"]),
        "bv": by_partition(inputs["L0_attn_bv"]),
        "bo": np.ascontiguousarray(inputs["L0_attn_bo"]),
        "wT": transposed(inputs["L0_ffn_weight"]),
        "a1T": transposed(inputs["L0_ffn_aux_weight1"]),
        "a2": np.ascontiguousarray(inputs["L0_ffn_aux_weight2"]),
        "bf": np.ascontiguousarray(inputs["L0_ffn_bias"]),
    }
    nc = bacc.Bacc("TRN2", target_bir_lowering=False, num_devices=1)
    aps = [nc.dram_tensor(n, a.shape, mybir.dt.from_np(a.dtype), kind="ExternalInput").ap()
           for n, a in arrays.items()]
    out = nc.dram_tensor("out", arrays["x"].shape, mybir.dt.float32, kind="ExternalOutput").ap()
    linear_attention_ffn_kernel(nc, *aps, out)
    result = run_bass_kernel_spmd(nc, [arrays], core_ids=[0])
    return result.results[0]["out"]
```
